# Optimizing a Trainium2 kernel written in Bass

```python
import numpy as np
import jax
import jax.numpy as jnp

def _softmax(x, axis=-1):
    return jax.nn.softmax(x, axis=axis)

def _gelu(x):
    return jax.nn.gelu(x, approximate=True)

def _silu(x):
    return jax.nn.silu(x)

def _sigmoid(x):
    return jax.nn.sigmoid(x)

def _layernorm(x, axis=-1, eps=1e-05):
    m = jnp.mean(x, axis=axis, keepdims=True)
    v = jnp.var(x, axis=axis, keepdims=True)
    return (x - m) / jnp.sqrt(v + eps)

def _scatter_add(tgt, idx, src, axis=0):
    return tgt.at[idx].add(src)

def _segment_sum(src, seg, n):
    return jax.ops.segment_sum(src, seg, n)
kernel_name = 'mk_recurrent_d1_jaxref_r8_241f96'

def setup_inputs(seed: int=0):
    np.random.seed(seed)
    _w = jnp.asarray

    def _L0_attn_setup():
        import jax, jax.numpy as jnp
        import numpy as np
        H = 512
        D = H // 4
        key = jax.random.key(seed)
        k1, k2, k3, k4, k5 = jax.random.split(key, 5)
        x = jax.random.normal(k1, (4, 512, H), dtype=jnp.float32)
        s_in = 1.0 / np.sqrt(H)
        Wqkv = jax.random.normal(k2, (H, 3 * D), dtype=jnp.float32) * s_in
        bqkv = jax.random.normal(k3, (3 * D,), dtype=jnp.float32) * 0.01
        Wo = jax.random.normal(k4, (D, H), dtype=jnp.float32) * (1.0 / np.sqrt(D))
        bo = jax.random.normal(k5, (H,), dtype=jnp.float32) * 0.01
        return {'x': x, 'Wqkv': Wqkv, 'bqkv': bqkv, 'Wo': Wo, 'bo': bo}
    _L0_attn_in = _L0_attn_setup()

    def _L0_ffn_setup():
        import jax, jax.numpy as jnp
        import numpy as np
        H = 512
        I = 1792
        G = 128

        def dequant(q, s, g=G):
            O, In = q.shape
            return (q.reshape(O, In // g, g).astype(s.dtype) * s[:, :, None]).reshape(O, In)
        key = jax.random.key(seed)
        ks = jax.random.split(key, 7)
        x = jax.random.normal(ks[0], (2, 256, H), dtype=jnp.float32)

        def mk_qlinear(kq, ksc, out_d, in_d):
            q = jax.random.randint(kq, (out_d, in_d), -8, 8, dtype=jnp.int32)
            s = jax.random.uniform(ksc, (out_d, in_d // G), dtype=jnp.float32, minval=0.005, maxval=0.02)
            return (q, s)
        gate_q, gate_s = mk_qlinear(ks[1], ks[2], I, H)
        up_q, up_s = mk_qlinear(ks[3], ks[4], I, H)
        down_q, down_s = mk_qlinear(ks[5], ks[6], H, I)
        return {'x': x, 'gate_q': gate_q, 'gate_s': gate_s, 'up_q': up_q, 'up_s': up_s, 'down_q': down_q, 'down_s': down_s}
    _L0_ffn_in = _L0_ffn_setup()
    _d = {'L0_attn_x': _L0_attn_in['x'], 'L0_attn_Wqkv': _L0_attn_in['Wqkv'], 'L0_attn_bqkv': _L0_attn_in['bqkv'], 'L0_attn_Wo': _L0_attn_in['Wo'], 'L0_attn_bo': _L0_attn_in['bo'], 'L0_ffn_gate_q': _L0_ffn_in['gate_q'], 'L0_ffn_gate_s': _L0_ffn_in['gate_s'], 'L0_ffn_up_q': _L0_ffn_in['up_q'], 'L0_ffn_up_s': _L0_ffn_in['up_s'], 'L0_ffn_down_q': _L0_ffn_in['down_q'], 'L0_ffn_down_s': _L0_ffn_in['down_s']}
    _x0 = _d['L0_attn_x']
    _d['L0_attn_x'] = jax.random.normal(jax.random.fold_in(jax.random.key(seed), 1), (1, 2048, 512), dtype=_x0.dtype)
    del _x0
    return _d

def reference(L0_attn_x, L0_attn_Wqkv, L0_attn_bqkv, L0_attn_Wo, L0_attn_bo, L0_ffn_gate_q, L0_ffn_gate_s, L0_ffn_up_q, L0_ffn_up_s, L0_ffn_down_q, L0_ffn_down_s):

    def _L0_attn_ref(x, Wqkv, bqkv, Wo, bo):
        import jax, jax.numpy as jnp
        import numpy as np
        H = 512
        D = H // 4
        B, S, C = x.shape
        d = C // 4
        qkv = jnp.einsum('bsc,cf->bsf', x, Wqkv) + bqkv
        qkv = qkv.reshape(B, S, 3, d)
        q, k, v = (qkv[:, :, 0], qkv[:, :, 1], qkv[:, :, 2])
        scale = 1.0 / jnp.sqrt(jnp.float32(d)).astype(x.dtype)
        attn = jnp.einsum('bqd,bkd->bqk', q, k) * scale
        attn = jax.nn.softmax(attn, axis=-1)
        out = jnp.einsum('bqk,bkd->bqd', attn, v)
        return jnp.einsum('bqd,dc->bqc', out, Wo) + bo

    def _L0_ffn_ref(x, gate_q, gate_s, up_q, up_s, down_q, down_s):
        import jax, jax.numpy as jnp
        import numpy as np
        H = 512
        I = 1792
        G = 128

        def dequant(q, s, g=G):
            O, In = q.shape
            return (q.reshape(O, In // g, g).astype(s.dtype) * s[:, :, None]).reshape(O, In)
        Wg = dequant(gate_q, gate_s)
        Wu = dequant(up_q, up_s)
        Wd = dequant(down_q, down_s)
        gate_score = jax.nn.silu(jnp.einsum('bsh,ih->bsi', x, Wg))
        intermediate = gate_score * jnp.einsum('bsh,ih->bsi', x, Wu)
        return jnp.einsum('bsi,hi->bsh', intermediate, Wd)
    x = L0_attn_x
    xn = _layernorm(x, axis=-1)
    s = _L0_attn_ref(xn, L0_attn_Wqkv, L0_attn_bqkv, L0_attn_Wo, L0_attn_bo)
    g = _silu(_L0_ffn_ref(xn, L0_ffn_gate_q, L0_ffn_gate_s, L0_ffn_up_q, L0_ffn_up_s, L0_ffn_down_q, L0_ffn_down_s))
    x = x + s * g
    return x

_drawn_inputs = setup_inputs


def setup_inputs(seed=0):
    import zlib

    import numpy as np

    out = dict(_drawn_inputs(seed))
    spreads = {}
    factors = {'L0_attn_bo': 2.688}
    for name, (base, spread) in spreads.items():
        noise = np.random.default_rng([zlib.crc32(name.encode()), seed]).standard_normal(out[name].shape)
        drawn = base * np.exp(spread * noise) if base else spread * noise
        out[name] = jnp.asarray(drawn.astype(out[name].dtype))
    for name, factor in factors.items():
        out[name] = (out[name] * factor).astype(out[name].dtype)
    return out
```

```python
from contextlib import ExitStack

import concourse.bass as bass
from concourse import mybir

F32 = mybir.dt.float32
F16 = mybir.dt.float16
BF16 = mybir.dt.bfloat16
I32 = mybir.dt.int32
ALU = mybir.AluOpType
ACT = mybir.ActivationFunctionType
AX_X = mybir.AxisListType.X
AX_XY = mybir.AxisListType.XY
ABSMAX = bass.bass_isa.ReduceOp.absmax

P = 128
ROWS = 2048
HID = 512
D = HID // 4
INNER = 1792
LN_EPS = 1e-5

HT = HID // P
OT = INNER // P
RT = ROWS // P
CHUNK = 512
NC = ROWS // CHUNK
TPC = CHUNK // P
HALF = 1024
NH = ROWS // HALF

X_EXP = 11
X_SCALE = float(2 ** X_EXP)
PROB_EXP = 8
SHIFT_EXP = 22
LN2 = 0.6931471805599453
QKV_L1 = 512.0
FFN_L1 = 4096.0
SCALE_BITS = float((127 + 14 + 127) << 23)
INVERSE_BITS = float((127 + 127) << 23)

FULL = [("g", 0), ("u", 0), ("y", 0), ("g", 1), ("u", 1), ("y", 1),
        ("g", 2), ("u", 2), ("y", 2), ("g", 3), ("u", 3), ("y", 3)]
OPEN = [x for x in FULL if x[0] != "y"]
CLOSE = [x for x in FULL if x[0] == "y"]
ACT_DRAINS = [("g", 0), ("u", 0), ("y", 1), ("y", 2), ("y", 3)]
DVE_DRAINS = [x for x in FULL if x not in ACT_DRAINS]
RING = 4
STEPS = NH * OT


def before(step, of, opening):
    if isinstance(step, int) and step <= 2:
        return opening * step
    return (step - 2) * of + 2 * opening


def products_before(step):
    return before(step, len(FULL), len(OPEN))


def act_drains_before(step):
    return before(step, len(ACT_DRAINS), 2)


def dve_drains_before(step):
    return before(step, len(DVE_DRAINS), 6)


def build(nc, x, xT, wqkv, bqkv, wo, bo, gate_q, gate_s, up_q, up_s, down_q, down_s, outT):
    ctx = ExitStack()
    with ctx:
        def sb(name, shape, dt, scope=ctx):
            return scope.enter_context(nc.sbuf_tensor(name, shape, dt))

        def pb(name, shape, dt, scope=ctx):
            return scope.enter_context(nc.psum_tensor(name, shape, dt))

        def sem(name):
            return ctx.enter_context(nc.semaphore(name))

        gate16 = sb("gate16", [P, HT, INNER], F16)
        up16 = sb("up16", [P, HT, INNER], F16)
        down16 = sb("down16", [P, OT, HID], F16)
        xnT = sb("xnT", [P, 2, HT, ROWS], F16)
        attnT = sb("attnT", [P, HT, ROWS], F32)
        gate_col = sb("gate_col", [P, OT, HT], F32)
        up_col = sb("up_col", [P, OT, HT], F32)
        down_col = sb("down_col", [P, HT, OT], F32)
        gate_dq = sb("gate_dq", [P, OT, HT], F32)
        up_dq = sb("up_dq", [P, OT, HT], F32)
        down_dq = sb("down_dq", [P, HT, OT], F32)
        bo_col = sb("bo_col", [P, HT], F32)
        bqkv_col = sb("bqkv_col", [P, 3], F32)
        bqkv_sc = sb("bqkv_sc", [P, 3], F32)
        ident = sb("ident", [P, P], F16)
        ones16 = sb("ones16", [P, P], F16)
        shift_up = sb("shift_up", [P, P], BF16)
        exp_bias = sb("exp_bias", [P, 1], F32)
        absmax = sb("absmax", [P, 5], F32)
        absmax_all = sb("absmax_all", [P, 5], F32)
        bound = sb("bound", [P, 4], F32)
        fit = sb("fit", [P, 4], F32)
        unfit = sb("unfit", [P, 4], F32)
        qkv_unscale = sb("qkv_unscale", [P, 1], F32)
        exp_scale = sb("exp_scale", [P, 1], F32)
        attn_unscale = sb("attn_unscale", [P, 1], F32)
        up_factor = sb("up_factor", [P, 1], F32)

        rows_scope = ExitStack()
        x_rows = sb("x_rows", [P, RT, HID], F32, rows_scope)
        rows_scope.close()
        ysum = sb("ysum", [P, HT, ROWS], F32)

        att = ExitStack()
        q16 = sb("q16", [P, 2, ROWS], F16, att)
        k16 = sb("k16", [P, 2, ROWS], F16, att)
        v16 = sb("v16", [P, 2, RT, D], F16, att)
        wo16 = sb("wo16", [P, 2, HID], F16, att)
        wqkv16 = sb("wqkv16", [P, 2, HT, 3 * D], F16, att)
        ln = ExitStack()
        wqkv32 = sb("wqkv32", [P, HT, 3 * D], F32, ln)
        wo32 = sb("wo32", [P, HID], F32, ln)
        xn32 = sb("xn32", [P, TPC, HID], F32, ln)
        xn16 = sb("xn16", [P, TPC, 2, HID], F16, ln)
        qkv32 = sb("qkv32", [P, 3, CHUNK], F32, ln)
        bn6 = sb("bn6", [P, TPC, 6], F32, ln)
        mean_var = sb("mean_var", [P, TPC, 2], F32, ln)
        var_eps = sb("var_eps", [P, TPC], F32, ln)
        std = sb("std", [P, TPC], F32, ln)
        rstd0 = sb("rstd0", [P, TPC], F32, ln)
        newton = sb("newton", [P, TPC], F32, ln)
        newton2 = sb("newton2", [P, TPC], F32, ln)
        newton3 = sb("newton3", [P, TPC], F32, ln)
        x_mul = sb("x_mul", [P, TPC], F32, ln)
        x_add = sb("x_add", [P, TPC], F32, ln)
        ln.close()
        p32 = sb("p32", [P, 4, CHUNK], F32, att)
        p16 = sb("p16", [P, 4, 2, CHUNK], F16, att)
        p_sum = sb("p_sum", [P, CHUNK], F32, att)
        p_sum16 = sb("p_sum16", [P, 2, CHUNK], F16, att)
        neg_max = sb("neg_max", [P, CHUNK], F16, att)
        max_parts = sb("max_parts", [P, TPC, 4], F32, att)
        max_col = sb("max_col", [P, TPC], F32, att)
        o_raw = sb("o_raw", [P, CHUNK], F32, att)
        o_norm = sb("o_norm", [P, CHUNK], F32, att)
        o32 = sb("o32", [P, CHUNK], F32, att)
        o16 = sb("o16", [P, 2, CHUNK], F16, att)
        inv_sum = sb("inv_sum", [P, CHUNK], F32, att)
        att.close()

        ffn = ExitStack()
        g32 = sb("g32", [P, 2, HALF], F32, ffn)
        u32 = sb("u32", [P, 2, HALF], F32, ffn)
        silu32 = sb("silu32", [P, HALF], F32, ffn)
        h32 = sb("h32", [P, 2, HALF], F32, ffn)
        h16 = sb("h16", [P, 2, 2, HALF], F16, ffn)
        y_part = sb("y_part", [P, 3, HALF], F32, ffn)
        x_res = sb("x_res", [P, 2, HALF], F32, ffn)
        out32 = sb("out32", [P, 2, HALF], F32, ffn)
        ffn.close()

        front = ExitStack()
        xn_ps = pb("xn_ps", [P, TPC, 2, HT, P], F16, front)
        qkv_ps = pb("qkv_ps", [P, 3, CHUNK], F32, front)
        front.close()
        attps = ExitStack()
        score_ps = pb("score_ps", [P, 4, CHUNK], F32, attps)
        o_ps = pb("o_ps", [P, CHUNK], F32, attps)
        max_ps = pb("max_ps", [P, 2, CHUNK], F32, attps)
        tail_ps = pb("tail_ps", [P, CHUNK], F32, attps)
        attps.close()
        ffn_ps = pb("ffn_ps", [P, RING, 2, CHUNK], F32)

        names = """x_landed weights_landed wo_landed scales_landed residual_landed int4_landed
            out_stored identity_zeroed identity_ready consts_ready absmax_ready absmax_spread
            scales_ready scaled_w w16_hi w16_ready wo16_hi
            var_ready std_ready moments_ready xn32_ready xn_hi_ready xn_lo_ready xn_transposed
            xn_stored q_product k_product v_product qkv32_ready qkv_hi_ready qkv_lo_ready
            max_product max_reduced shift_ready score_product exp32_done exp16_done p_lo_ready
            pv_product p_summed max_done sum_inverted dve_moments sum_hi_ready sum_split sum_spread o_copied o_scaled o32_ready
            o_hi_ready o_lo_ready attn_product attn_stored dve_small
            ysum_zeroed ffn_product act_drained dve_drained silu_done h_ready h_hi_ready h_lo_ready
            y_added final_silu final_scaled final_ready""".split()
        s = {n: sem(n) for n in names}

        block = ctx.enter_context(nc.Block())

        @block.sync
        def _(sp):
            xv = x.rearrange("(t p) h -> p t h", p=P)
            for c in range(NC):
                if c:
                    sp.wait_ge(s["x_landed"], 16 * c)
                sp.dma_start(x_rows[:, c * TPC:(c + 1) * TPC, :],
                             xv[:, c * TPC:(c + 1) * TPC, :]).then_inc(s["x_landed"], 16)
            xTv = xT.rearrange("(j p) r -> p j r", p=P)
            outv = outT.rearrange("(j p) r -> p j r", p=P)
            sp.wait_ge(s["attn_stored"], NC * HT)
            for n in range(NH * HT):
                rows = slice((n // HT) * HALF, (n // HT + 1) * HALF)
                if n:
                    sp.wait_ge(s["residual_landed"], 16 * n)
                if n >= 2:
                    sp.wait_ge(s["final_ready"], n - 1)
                sp.dma_start(x_res[:, n % 2, :], xTv[:, n % HT, rows]).then_inc(s["residual_landed"], 16)
                if n >= 2:
                    m = n - 2
                    if m:
                        sp.wait_ge(s["out_stored"], 16 * m)
                    rows = slice((m // HT) * HALF, (m // HT + 1) * HALF)
                    sp.dma_start(outv[:, m % HT, rows], out32[:, m % 2, :]).then_inc(s["out_stored"], 16)
            for m in range(NH * HT - 2, NH * HT):
                rows = slice((m // HT) * HALF, (m // HT + 1) * HALF)
                sp.wait_ge(s["final_ready"], m + 1)
                sp.wait_ge(s["out_stored"], 16 * m)
                sp.dma_start(outv[:, m % HT, rows], out32[:, m % 2, :]).then_inc(s["out_stored"], 16)
            sp.wait_ge(s["out_stored"], 16 * NH * HT)

        @block.gpsimd
        def _(pool):
            nc.gpsimd.memset(ident[:], 0.0).then_inc(s["identity_zeroed"], 1)
            nc.gpsimd.memset(ones16[:], 1.0)
            nc.gpsimd.memset(shift_up[:], float(2 ** SHIFT_EXP))
            nc.gpsimd.memset(exp_bias[:], PROB_EXP * LN2).then_inc(s["consts_ready"], 1)
            pool.wait_ge(s["identity_zeroed"], 1)
            nc.gpsimd.affine_select(out=ident[:], in_=ident[:], compare_op=ALU.not_equal, fill=1.0,
                                    base=0, pattern=[[-1, P]], channel_multiplier=1
                                    ).then_inc(s["identity_ready"], 1)
            pool.wait_ge(s["absmax_ready"], 1)
            nc.gpsimd.partition_all_reduce(absmax_all[:], absmax[:], P, ABSMAX
                                           ).then_inc(s["absmax_spread"], 1)

            def normalise(c):
                pool.wait_ge(s["moments_ready"], c + 1)
                if isinstance(c, int) and c == 0:
                    pool.wait_ge(s["x_landed"], 16)
                else:
                    pool.wait_ge(s["xn_lo_ready"], c * TPC)
                    pool.wait_ge(s["xn_transposed"], c * TPC)
                for t in range(TPC):
                    row = x_rows[:, bass.ds(c * TPC + t, 1), :].rearrange("p a h -> p (a h)")
                    nc.gpsimd.tensor_scalar(xn32[:, t, :], row, x_mul[:, t:t + 1], x_add[:, t:t + 1],
                                            ALU.mult, ALU.add).then_inc(s["xn32_ready"], 1)
                    nc.gpsimd.tensor_scalar(xn16[:, t, 0, :], row, x_mul[:, t:t + 1], x_add[:, t:t + 1],
                                            ALU.mult, ALU.add).then_inc(s["xn_hi_ready"], 1)

            for c in range(NC):
                normalise(c)
            for dst, src in ((gate16, gate_q), (up16, up_q), (down16, down_q)):
                pool.dma_start(dst[:], src).then_inc(s["int4_landed"], 16)
            pool.wait_ge(s["xn_hi_ready"], RT)
            nc.gpsimd.memset(ysum[:], 0.0).then_inc(s["ysum_zeroed"], 1)

            def sum_probabilities(n):
                for k in range(1, RT):
                    pool.wait_ge(s["exp32_done"], n * RT + k + 1)
                    if k == 1:
                        if not (isinstance(n, int) and n == 0):
                            pool.wait_ge(s["sum_split"], n)
                        first = p32[:, 0, :]
                    else:
                        pool.wait_ge(s["p_summed"], n * (RT - 1) + k - 1)
                        first = p_sum[:]
                    nc.gpsimd.tensor_tensor(p_sum[:], first, p32[:, k % 4, :], ALU.add
                                            ).then_inc(s["p_summed"], 1)

            sum_probabilities(0)
            with pool.Fori(1, NC) as n:
                sum_probabilities(n)

            def ffn_step(t, parity, with_y, half):
                rows = slice(half * HALF, (half + 1) * HALF)

                def add(j):
                    pool.wait_ge(s["act_drained"], act_drains_before(t) + 2 * (not CLOSING[0]) + j)
                    if not (isinstance(t, int) and t == 2):
                        pool.wait_ge(s["y_added"], (t - 3) * 3 + j)
                    nc.gpsimd.tensor_tensor(ysum[:, j, rows], ysum[:, j, rows], y_part[:, j - 1, :],
                                            ALU.add).then_inc(s["y_added"], 1)

                if with_y:
                    add(1)
                if parity is not None:
                    pool.wait_ge(s["h_hi_ready"], t)
                    nc.gpsimd.tensor_tensor(h16[:, parity, 1, :], h32[:, parity, :],
                                            h16[:, parity, 0, :], ALU.subtract
                                            ).then_inc(s["h_lo_ready"], 1)
                if with_y:
                    add(2)
                    add(3)

            CLOSING = [False]
            ffn_step(1, 0, False, 0)
            for half in range(NH):
                if half == 0:
                    ffn_step(2, 1, True, 0)
                    ffn_step(3, 0, True, 0)
                    first_pair = 2
                else:
                    ffn_step(half * OT, 1, True, half - 1)
                    ffn_step(half * OT + 1, 0, True, half - 1)
                    first_pair = half * (OT // 2) + 1
                with pool.Fori(first_pair, (half + 1) * (OT // 2)) as pair:
                    ffn_step(pair * 2, 1, True, half)
                    ffn_step(pair * 2 + 1, 0, True, half)
            CLOSING[0] = True
            for t in (STEPS, STEPS + 1):
                for j in (1, 2, 3):
                    pool.wait_ge(s["act_drained"], act_drains_before(STEPS) + 3 * (t - STEPS) + j)
                    pool.wait_ge(s["y_added"], (t - 3) * 3 + j)
                    if t == STEPS and j == 2:
                        pool.wait_ge(s["h_hi_ready"], STEPS)
                        nc.gpsimd.tensor_tensor(h16[:, 1, 1, :], h32[:, 1, :], h16[:, 1, 0, :],
                                                ALU.subtract).then_inc(s["h_lo_ready"], 1)
                    rows = slice((NH - 1) * HALF, NH * HALF)
                    nc.gpsimd.tensor_tensor(ysum[:, j, rows], ysum[:, j, rows], y_part[:, j - 1, :],
                                            ALU.add).then_inc(s["y_added"], 1)

        @block.scalar
        def _(act):
            act.dma_start(wqkv32[:], wqkv.rearrange("(i p) f -> p i f", p=P)
                          ).then_inc(s["weights_landed"], 16)
            act.dma_start(bqkv_col[:], bqkv).then_inc(s["scales_landed"], 16)
            act.dma_start(gate_col[:], gate_s).then_inc(s["scales_landed"], 16)
            act.dma_start(up_col[:], up_s).then_inc(s["scales_landed"], 16)
            act.dma_start(wo32[:], wo).then_inc(s["wo_landed"], 16)
            act.dma_start(bo_col[:], bo).then_inc(s["scales_landed"], 16)
            act.dma_start(down_col[:], down_s).then_inc(s["scales_landed"], 16)

            def square_root(c):
                act.wait_ge(s["var_ready"], c + 1)
                nc.scalar.activation(std[:], var_eps[:], ACT.Sqrt).then_inc(s["std_ready"], 1)

            def store_transposed(c):
                for t in range(TPC):
                    act.wait_ge(s["xn_transposed"], c * TPC + t + 1)
                    nc.scalar.activation(xnT[:, :, :, bass.ds(c * CHUNK + t * P, P)],
                                         xn_ps[:, t, :, :, :], ACT.Copy).then_inc(s["xn_stored"], 1)

            def store_qkv(c):
                first = isinstance(c, int) and c == 0
                for i, (product, dst) in enumerate((("q_product", q16), ("k_product", k16))):
                    act.wait_ge(s[product], c + 1)
                    if not first:
                        act.wait_ge(s["qkv_lo_ready"], c * 3 - 2 + i)
                    args = dict(scale=qkv_unscale[:, 0:1], bias=bqkv_sc[:, i:i + 1])
                    nc.scalar.activation(qkv32[:, i, :], qkv_ps[:, i, :], ACT.Identity, **args
                                         ).then_inc(s["qkv32_ready"], 1)
                    nc.scalar.activation(dst[:, 0, bass.ds(c * CHUNK, CHUNK)], qkv_ps[:, i, :],
                                         ACT.Identity, **args).then_inc(s["qkv_hi_ready"], 1)
                act.wait_ge(s["v_product"], c + 1)
                if not first:
                    act.wait_ge(s["qkv_lo_ready"], c * 3)
                nc.scalar.activation(qkv32[:, 2, :], qkv_ps[:, 2, :], ACT.Copy,
                                     scale=qkv_unscale[:, 0:1]).then_inc(s["qkv32_ready"], 1)
                nc.scalar.activation(v16[:, 0, bass.ds(c * TPC, TPC), :],
                                     qkv_ps[:, 2, :].rearrange("p (t d) -> p t d", d=D), ACT.Copy,
                                     scale=qkv_unscale[:, 0:1]).then_inc(s["qkv_hi_ready"], 1)

            square_root(0)
            act.wait_ge(s["scaled_w"], 1)
            nc.scalar.activation(wqkv16[:, 0, :, :], wqkv32[:], ACT.Copy).then_inc(s["w16_hi"], 1)
            act.wait_ge(s["scaled_w"], 2)
            nc.scalar.activation(wo16[:, 0, :], wo32[:], ACT.Copy).then_inc(s["wo16_hi"], 1)
            store_transposed(0)
            square_root(1)
            store_transposed(1)
            store_qkv(0)
            with act.Fori(1, NC - 1) as c:
                square_root(c + 1)
                store_transposed(c + 1)
                store_qkv(c)
            store_qkv(NC - 1)

            act.wait_ge(s["consts_ready"], 1)

            def exponentials(n, k):
                act.wait_ge(s["score_product"], n * RT + k + 1)
                first = isinstance(n, int) and n == 0
                if not first or k >= 4:
                    act.wait_ge(s["p_lo_ready"], n * RT + k - 3)
                    if k >= 4:
                        act.wait_ge(s["p_summed"], n * (RT - 1) + max(k - 4, 1))
                    else:
                        act.wait_ge(s["p_summed"], n * (RT - 1) + k - 3)
                    act.wait_ge(s["pv_product"], n * RT + k - 3)
                args = dict(scale=exp_scale[:, 0:1], bias=exp_bias[:, 0:1])
                nc.scalar.activation(p32[:, k % 4, :], score_ps[:, k % 4, :], ACT.Exp, **args
                                     ).then_inc(s["exp32_done"], 1)
                nc.scalar.activation(p16[:, k % 4, 0, :], score_ps[:, k % 4, :], ACT.Exp, **args
                                     ).then_inc(s["exp16_done"], 1)

            def copy_o(m):
                act.wait_ge(s["pv_product"], (m + 1) * RT)
                if not (isinstance(m, int) and m == 0):
                    act.wait_ge(s["o_scaled"], m)
                nc.scalar.activation(o_raw[:], o_ps[:], ACT.Copy).then_inc(s["o_copied"], 1)

            def add_v_bias(m):
                act.wait_ge(s["o_scaled"], m + 1)
                if not (isinstance(m, int) and m == 0):
                    act.wait_ge(s["o_lo_ready"], m)
                    act.wait_ge(s["attn_product"], m * HT)
                args = dict(bias=bqkv_sc[:, 2:3])
                nc.scalar.activation(o32[:], o_norm[:], ACT.Identity, **args).then_inc(s["o32_ready"], 1)
                nc.scalar.activation(o16[:, 0, :], o_norm[:], ACT.Identity, **args
                                     ).then_inc(s["o_hi_ready"], 1)

            def store_attention(m, j):
                act.wait_ge(s["attn_product"], m * HT + j + 1)
                nc.scalar.activation(attnT[:, j, bass.ds(m * CHUNK, CHUNK)], tail_ps[:], ACT.Identity,
                                     scale=attn_unscale[:, 0:1], bias=bo_col[:, j:j + 1]
                                     ).then_inc(s["attn_stored"], 1)

            def attention(n, with_tail):
                for k in range(RT):
                    exponentials(n, k)
                    if with_tail:
                        if k == 1:
                            copy_o(n - 1)
                        if k == 8:
                            add_v_bias(n - 1)
                        if 11 <= k < 11 + HT:
                            store_attention(n - 1, k - 11)

            attention(0, False)
            with act.Fori(1, NC) as n:
                attention(n, True)
            copy_o(NC - 1)
            add_v_bias(NC - 1)
            for j in range(HT):
                store_attention(NC - 1, j)

            def drain(t, order, item, dst, scale):
                act.wait_ge(s["ffn_product"], products_before(t) + order.index(item) + 1)
                src = ffn_ps[:, order.index(item) % RING, :, :]
                nc.scalar.activation(dst.rearrange("p (a b) -> p a b", b=CHUNK), src, ACT.Copy,
                                     scale=scale).then_inc(s["act_drained"], 1)

            def silu_of(t, parity):
                act.wait_ge(s["dve_drained"], dve_drains_before(t + 1) - 1)
                if not (isinstance(t, int) and t == 0):
                    act.wait_ge(s["h_ready"], t)
                nc.scalar.activation(silu32[:], g32[:, parity, :], ACT.Silu).then_inc(s["silu_done"], 1)

            def h_hi(t, parity):
                act.wait_ge(s["h_ready"], t + 1)
                if not (isinstance(t, int) and t < 2):
                    act.wait_ge(s["ffn_product"], products_before(t + 1))
                nc.scalar.activation(h16[:, parity, 0, :], h32[:, parity, :], ACT.Copy
                                     ).then_inc(s["h_hi_ready"], 1)

            def y_drain(t, order, tile, j):
                if not (isinstance(t, int) and t == 2):
                    act.wait_ge(s["y_added"], (t - 3) * 3 + j)
                drain(t, order, ("y", j), y_part[:, j - 1, :], down_dq[:, j, bass.ds(tile, 1)])

            def ffn_step(t, parity, tile, y_tile):
                order = OPEN if y_tile is None else FULL
                if not (isinstance(t, int) and t == 0):
                    silu_of(t - 1, 1 - parity)
                if not (isinstance(t, int) and t < 2):
                    act.wait_ge(s["h_ready"], t - 1)
                drain(t, order, ("g", 0), g32[:, parity, :], gate_dq[:, bass.ds(tile, 1), 0])
                drain(t, order, ("u", 0), u32[:, parity, :], up_dq[:, bass.ds(tile, 1), 0])
                if y_tile is not None:
                    y_drain(t, order, y_tile, 1)
                if not (isinstance(t, int) and t == 0):
                    h_hi(t - 1, 1 - parity)
                if y_tile is not None:
                    y_drain(t, order, y_tile, 2)
                    y_drain(t, order, y_tile, 3)

            def final(half):
                rows = slice(half * HALF, (half + 1) * HALF)
                for j in range(HT):
                    m = half * HT + j
                    if j == 0:
                        act.wait_ge(s["dve_drained"], dve_drains_before((half + 1) * OT) + 7 + 1
                                    if half < NH - 1 else dve_drains_before(STEPS) + 2)
                    else:
                        act.wait_ge(s["y_added"], 3 * ((half + 1) * OT - 1) + j)
                    nc.scalar.activation(ysum[:, j, rows], ysum[:, j, rows], ACT.Silu
                                         ).then_inc(s["final_silu"], 1)

            act.wait_ge(s["o_lo_ready"], NC)
            act.wait_ge(s["p_summed"], NC * (RT - 1))
            act.wait_ge(s["attn_stored"], NC * HT)
            ffn_step(0, 0, 0, None)
            ffn_step(1, 1, 1, None)
            for half in range(NH):
                h2 = OT // 2
                if half == 0:
                    ffn_step(2, 0, 2, 0)
                    ffn_step(3, 1, 3, 1)
                    first_pair = 2
                else:
                    ffn_step(half * OT, 0, 0, OT - 2)
                    ffn_step(half * OT + 1, 1, 1, OT - 1)
                    final(half - 1)
                    first_pair = half * h2 + 1
                with act.Fori(first_pair, (half + 1) * h2) as pair:
                    ffn_step(pair * 2, 0, pair * 2 - half * OT, pair * 2 - half * OT - 2)
                    ffn_step(pair * 2 + 1, 1, pair * 2 - half * OT + 1, pair * 2 - half * OT - 1)
            silu_of(STEPS - 1, 1)
            for t in (STEPS, STEPS + 1):
                for j in (1, 2, 3):
                    if t == STEPS and j == 2:
                        h_hi(STEPS - 1, 1)
                    act.wait_ge(s["y_added"], (t - 3) * 3 + j)
                    act.wait_ge(s["ffn_product"], products_before(STEPS) + 4 * (t - STEPS) + j + 1)
                    nc.scalar.activation(y_part[:, j - 1, :].rearrange("p (a b) -> p a b", b=CHUNK),
                                         ffn_ps[:, j, :, :], ACT.Copy,
                                         scale=down_dq[:, j, OT - 2 + t - STEPS:OT - 1 + t - STEPS]
                                         ).then_inc(s["act_drained"], 1)
            final(NH - 1)

        @block.vector
        def _(dve):
            small = [0]

            def chain(op):
                small[0] += 1
                op.then_inc(s["dve_small"], 1)
                dve.wait_ge(s["dve_small"], small[0])

            def moments(c, in_loop_at=None):
                first = isinstance(c, int) and c == 0
                dve.wait_ge(s["x_landed"], c * 16 + 16)
                count = [0]

                def link(op):
                    count[0] += 1
                    op.then_inc(s["dve_moments"], 1)
                    dve.wait_ge(s["dve_moments"], c * 8 + count[0])

                for t in range(TPC):
                    row = x_rows[:, bass.ds(c * TPC + t, 1), :].rearrange("p a h -> p (a h)")
                    last = nc.vector.bn_stats(bn6[:, t, :], row)
                link(last)
                nc.vector.memset(var_eps[:], LN_EPS)
                for t in range(TPC):
                    last = nc.vector.bn_aggr(mean_var[:, t, :], bn6[:, t, :])
                link(last)
                nc.vector.tensor_tensor(var_eps[:], mean_var[:, :, 1], var_eps[:], ALU.add
                                        ).then_inc(s["var_ready"], 1)
                dve.wait_ge(s["std_ready"], c + 1)
                link(nc.vector.reciprocal(rstd0[:], std[:]))
                link(nc.vector.tensor_tensor(newton[:], var_eps[:], rstd0[:], ALU.mult))
                link(nc.vector.tensor_tensor(newton2[:], newton[:], rstd0[:], ALU.mult))
                link(nc.vector.tensor_scalar(newton3[:], newton2[:], -0.5 * X_SCALE, 1.5 * X_SCALE,
                                             ALU.mult, ALU.add))
                if not first:
                    dve.wait_ge(s["xn_hi_ready"], c * TPC)
                link(nc.vector.tensor_tensor(x_mul[:], newton3[:], rstd0[:], ALU.mult))
                link(nc.vector.tensor_tensor(newton[:], mean_var[:, :, 0], x_mul[:], ALU.mult))
                nc.vector.tensor_scalar(x_add[:], newton[:], -1.0, None, ALU.mult
                                        ).then_inc(s["moments_ready"], 1)

            def split_xn(c):
                for t in range(TPC):
                    dve.wait_ge(s["xn_hi_ready"], c * TPC + t + 1)
                    nc.vector.tensor_tensor(xn16[:, t, 1, :], xn32[:, t, :], xn16[:, t, 0, :],
                                            ALU.subtract).then_inc(s["xn_lo_ready"], 1)

            def split_qkv(c):
                views = (q16[:, :, bass.ds(c * CHUNK, CHUNK)], k16[:, :, bass.ds(c * CHUNK, CHUNK)])
                for i, dst in enumerate(views):
                    dve.wait_ge(s["qkv_hi_ready"], c * 3 + i + 1)
                    nc.vector.tensor_tensor(dst[:, 1, :], qkv32[:, i, :], dst[:, 0, :],
                                            ALU.subtract).then_inc(s["qkv_lo_ready"], 1)
                dve.wait_ge(s["qkv_hi_ready"], c * 3 + 3)
                nc.vector.tensor_tensor(v16[:, 1, bass.ds(c * TPC, TPC), :],
                                        qkv32[:, 2, :].rearrange("p (t d) -> p t d", d=D),
                                        v16[:, 0, bass.ds(c * TPC, TPC), :],
                                        ALU.subtract).then_inc(s["qkv_lo_ready"], 1)

            dve.wait_ge(s["weights_landed"], 16)
            nc.vector.reduce_max(absmax[:, 0:1], wqkv32[:], AX_XY, apply_absolute_value=True)
            dve.wait_ge(s["wo_landed"], 16)
            nc.vector.reduce_max(absmax[:, 1:2], wo32[:], AX_X, apply_absolute_value=True)
            dve.wait_ge(s["scales_landed"], 5 * 16)
            nc.vector.reduce_max(absmax[:, 2:3], bqkv_col[:], AX_X, apply_absolute_value=True)
            nc.vector.reduce_max(absmax[:, 3:4], gate_col[:], AX_XY, apply_absolute_value=True)
            nc.vector.reduce_max(absmax[:, 4:5], up_col[:], AX_XY, apply_absolute_value=True
                                 ).then_inc(s["absmax_ready"], 1)
            moments(0)
            dve.wait_ge(s["absmax_spread"], 1)
            nc.vector.tensor_scalar(bound[:, 0:2], absmax_all[:, 0:2], 2.0 ** -20, None, ALU.max)
            chain(nc.vector.scalar_tensor_tensor(bound[:, 2:3], absmax_all[:, 0:1], QKV_L1,
                                                 absmax_all[:, 2:3], ALU.mult, ALU.add))
            chain(nc.vector.tensor_scalar(up_factor[:], absmax_all[:, 3:4], FFN_L1 * FFN_L1, None,
                                          ALU.mult))
            chain(nc.vector.tensor_tensor(bound[:, 3:4], up_factor[:], absmax_all[:, 4:5], ALU.mult))
            chain(nc.vector.tensor_scalar(bound[:, 2:4], bound[:, 2:4], 2.0 ** -20, None, ALU.max))
            chain(nc.vector.tensor_scalar(fit[:].bitcast(I32), bound[:].bitcast(I32), 0x7F800000, None,
                                          ALU.bitwise_and))
            chain(nc.vector.tensor_scalar(fit[:].bitcast(I32), fit[:].bitcast(I32), -1.0, SCALE_BITS,
                                          ALU.mult, ALU.add))
            chain(nc.vector.tensor_scalar(unfit[:].bitcast(I32), fit[:].bitcast(I32), -1.0,
                                          INVERSE_BITS, ALU.mult, ALU.add))
            nc.vector.tensor_scalar(wqkv32[:], wqkv32[:], fit[:, 0:1], None, ALU.mult
                                    ).then_inc(s["scaled_w"], 1)
            nc.vector.tensor_scalar(wo32[:], wo32[:], fit[:, 1:2], None, ALU.mult
                                    ).then_inc(s["scaled_w"], 1)
            nc.vector.tensor_scalar(qkv_unscale[:], unfit[:, 0:1], fit[:, 2:3], 1.0 / X_SCALE,
                                    ALU.mult, ALU.mult)
            nc.vector.tensor_scalar(bqkv_sc[:], bqkv_col[:], fit[:, 2:3], None, ALU.mult)
            chain(nc.vector.tensor_scalar(exp_scale[:], unfit[:, 2:3], unfit[:, 2:3], float(D) ** -0.5,
                                          ALU.mult, ALU.mult))
            nc.vector.tensor_tensor(attn_unscale[:], unfit[:, 1:2], unfit[:, 2:3], ALU.mult)
            nc.vector.tensor_scalar(gate_dq[:], gate_col[:], 1.0 / X_SCALE, None, ALU.mult)
            nc.vector.tensor_scalar(up_dq[:], up_col[:], fit[:, 3:4], 1.0 / X_SCALE, ALU.mult, ALU.mult)
            nc.vector.tensor_scalar(down_dq[:], down_col[:], unfit[:, 3:4], None, ALU.mult
                                    ).then_inc(s["scales_ready"], 1)
            dve.wait_ge(s["w16_hi"], 1)
            nc.vector.tensor_tensor(wqkv16[:, 1, :, :], wqkv32[:], wqkv16[:, 0, :, :], ALU.subtract
                                    ).then_inc(s["w16_ready"], 1)
            dve.wait_ge(s["wo16_hi"], 1)
            nc.vector.tensor_tensor(wo16[:, 1, :], wo32[:], wo16[:, 0, :], ALU.subtract
                                    ).then_inc(s["w16_ready"], 1)
            split_xn(0)
            with dve.Fori(0, NC - 1) as c:
                moments(c + 1)
                split_xn(c + 1)
                split_qkv(c)
            split_qkv(NC - 1)

            def reduce_scores(n, k):
                dve.wait_ge(s["max_product"], n * RT + k + 1)
                nc.vector.reduce_max(max_parts[:, k // 4, k % 4:k % 4 + 1], max_ps[:, k % 2, :], AX_X
                                     ).then_inc(s["max_reduced"], 1)

            def shift_of(n):
                dve.wait_ge(s["max_reduced"], (n + 1) * RT)
                nc.vector.reduce_max(max_col[:], max_parts[:], AX_X).then_inc(s["max_done"], 1)
                dve.wait_ge(s["max_done"], n + 1)
                if not (isinstance(n, int) and n == 0):
                    dve.wait_ge(s["score_product"], n * RT)
                for j in range(TPC):
                    last = nc.vector.tensor_scalar(neg_max[:, j * P:(j + 1) * P], ident[:],
                                                   max_col[:, j:j + 1], -(2.0 ** -SHIFT_EXP),
                                                   ALU.mult, ALU.mult)
                last.then_inc(s["shift_ready"], 1)

            def p_lo(n, k):
                dve.wait_ge(s["exp16_done"], n * RT + k + 1)
                nc.vector.tensor_tensor(p16[:, k % 4, 1, :], p32[:, k % 4, :], p16[:, k % 4, 0, :],
                                        ALU.subtract).then_inc(s["p_lo_ready"], 1)

            def split_sum(m):
                dve.wait_ge(s["p_summed"], (m + 1) * (RT - 1))
                if not (isinstance(m, int) and m == 0):
                    dve.wait_ge(s["sum_spread"], m)
                nc.vector.tensor_copy(p_sum16[:, 0, :], p_sum[:]).then_inc(s["sum_hi_ready"], 1)
                dve.wait_ge(s["sum_hi_ready"], m + 1)
                nc.vector.tensor_tensor(p_sum16[:, 1, :], p_sum[:], p_sum16[:, 0, :], ALU.subtract
                                        ).then_inc(s["sum_split"], 1)

            def invert_sum(m):
                dve.wait_ge(s["sum_spread"], m + 1)
                nc.vector.reciprocal(inv_sum[:], tail_ps[:]).then_inc(s["sum_inverted"], 1)

            def scale_o(m):
                dve.wait_ge(s["o_copied"], m + 1)
                dve.wait_ge(s["sum_inverted"], m + 1)
                if not (isinstance(m, int) and m == 0):
                    dve.wait_ge(s["o_hi_ready"], m)
                nc.vector.tensor_tensor(o_norm[:], o_raw[:], inv_sum[:], ALU.mult
                                        ).then_inc(s["o_scaled"], 1)

            def split_o(m):
                dve.wait_ge(s["o_hi_ready"], m + 1)
                nc.vector.tensor_tensor(o16[:, 1, :], o32[:], o16[:, 0, :], ALU.subtract
                                        ).then_inc(s["o_lo_ready"], 1)

            def attention(n, with_tail, with_next):
                for k in range(RT):
                    if with_next:
                        reduce_scores(n + 1, k)
                    p_lo(n, k)
                    if with_tail:
                        if k == 1:
                            split_sum(n - 1)
                        if k == 4:
                            invert_sum(n - 1)
                        if k == 6:
                            scale_o(n - 1)
                        if k == 9:
                            split_o(n - 1)
                if with_next:
                    shift_of(n + 1)

            dve.wait_ge(s["identity_ready"], 1)
            for k in range(RT):
                reduce_scores(0, k)
            shift_of(0)
            attention(0, False, True)
            with dve.Fori(1, NC - 1) as n:
                attention(n, True, True)
            attention(NC - 1, True, False)
            split_sum(NC - 1)
            invert_sum(NC - 1)
            scale_o(NC - 1)
            split_o(NC - 1)

            def accumulate(t, order, item, dst, scale):
                dve.wait_ge(s["ffn_product"], products_before(t) + order.index(item) + 1)
                dst = dst.rearrange("p (a b) -> p a b", b=CHUNK)
                nc.vector.scalar_tensor_tensor(dst, ffn_ps[:, order.index(item) % RING, :, :], scale,
                                               dst, ALU.mult, ALU.add).then_inc(s["dve_drained"], 1)

            def make_h(t, parity):
                dve.wait_ge(s["silu_done"], t + 1)
                dve.wait_ge(s["dve_drained"], dve_drains_before(t + 1))
                if not (isinstance(t, int) and t < 2):
                    dve.wait_ge(s["h_lo_ready"], t - 1)
                nc.vector.tensor_tensor(h32[:, parity, :], silu32[:], u32[:, parity, :], ALU.mult
                                        ).then_inc(s["h_ready"], 1)

            def ffn_step(t, parity, tile, y_tile, half):
                order = OPEN if y_tile is None else FULL
                done = dve_drains_before(t)
                if y_tile is not None:
                    rows = slice(half * HALF, (half + 1) * HALF)
                    if isinstance(t, int) and t == 2:
                        dve.wait_ge(s["ysum_zeroed"], 1)
                    else:
                        dve.wait_ge(s["dve_drained"], done - 6)
                    accumulate(t, order, ("y", 0), ysum[:, 0, rows], down_dq[:, 0, bass.ds(y_tile, 1)])
                    done = done + 1
                if not (isinstance(t, int) and t == 0):
                    make_h(t - 1, 1 - parity)
                for g in range(1, HT):
                    dve.wait_ge(s["act_drained"], act_drains_before(t) + 1) if g == 1 else \
                        dve.wait_ge(s["dve_drained"], done + 2 * g - 3)
                    accumulate(t, order, ("g", g), g32[:, parity, :], gate_dq[:, bass.ds(tile, 1), g])
                    dve.wait_ge(s["act_drained"], act_drains_before(t) + 2) if g == 1 else \
                        dve.wait_ge(s["dve_drained"], done + 2 * g - 2)
                    accumulate(t, order, ("u", g), u32[:, parity, :], up_dq[:, bass.ds(tile, 1), g])

            def final(half):
                rows = slice(half * HALF, (half + 1) * HALF)
                for j in range(HT):
                    m = half * HT + j
                    dve.wait_ge(s["final_silu"], m + 1)
                    nc.vector.tensor_tensor(ysum[:, j, rows], ysum[:, j, rows], attnT[:, j, rows],
                                            ALU.mult).then_inc(s["final_scaled"], 1)
                    dve.wait_ge(s["final_scaled"], m + 1)
                    dve.wait_ge(s["residual_landed"], 16 * (m + 1))
                    if m >= 2:
                        dve.wait_ge(s["out_stored"], 16 * (m - 1))
                    nc.vector.tensor_tensor(out32[:, m % 2, :], ysum[:, j, rows], x_res[:, m % 2, :],
                                            ALU.add).then_inc(s["final_ready"], 1)

            ffn_step(0, 0, 0, None, 0)
            ffn_step(1, 1, 1, None, 0)
            for half in range(NH):
                h2 = OT // 2
                if half == 0:
                    ffn_step(2, 0, 2, 0, 0)
                    ffn_step(3, 1, 3, 1, 0)
                    first_pair = 2
                else:
                    ffn_step(half * OT, 0, 0, OT - 2, half - 1)
                    ffn_step(half * OT + 1, 1, 1, OT - 1, half - 1)
                    final(half - 1)
                    first_pair = half * h2 + 1
                with dve.Fori(first_pair, (half + 1) * h2) as pair:
                    ffn_step(pair * 2, 0, pair * 2 - half * OT, pair * 2 - half * OT - 2, half)
                    ffn_step(pair * 2 + 1, 1, pair * 2 - half * OT + 1, pair * 2 - half * OT - 1, half)
            done = dve_drains_before(STEPS)
            rows = slice((NH - 1) * HALF, NH * HALF)
            for t in (STEPS, STEPS + 1):
                dve.wait_ge(s["ffn_product"], products_before(STEPS) + 4 * (t - STEPS) + 1)
                dve.wait_ge(s["dve_drained"], done - 6 if t == STEPS else done + 1)
                dst = ysum[:, 0, rows].rearrange("p (a b) -> p a b", b=CHUNK)
                nc.vector.scalar_tensor_tensor(dst, ffn_ps[:, 0, :, :],
                                               down_dq[:, 0, OT - 2 + t - STEPS:OT - 1 + t - STEPS],
                                               dst, ALU.mult, ALU.add).then_inc(s["dve_drained"], 1)
                if t == STEPS:
                    make_h(STEPS - 1, 1)
            final(NH - 1)

        @block.tensor
        def _(pe):
            def transpose_xn(c):
                for t in range(TPC):
                    if not (isinstance(c, int) and c == 0):
                        pe.wait_ge(s["xn_stored"], (c - 1) * TPC + t + 1)
                    pe.wait_ge(s["xn_lo_ready"], c * TPC + t + 1)
                    for part in range(2):
                        for i in range(HT):
                            last = nc.tensor.transpose(xn_ps[:, t, part, i, :],
                                                       xn16[:, t, part, i * P:(i + 1) * P], ident[:])
                    last.then_inc(s["xn_transposed"], 1)

            PAIRS = ((0, 0), (0, 1), (1, 0))

            def project(c):
                pe.wait_ge(s["xn_stored"], (c + 1) * TPC)
                for n, name in ((0, "q_product"), (1, "k_product")):
                    if not (isinstance(c, int) and c == 0):
                        pe.wait_ge(s["qkv_hi_ready"], c * 3 - 2 + n)
                    for i in range(HT):
                        for w, a in PAIRS:
                            last = nc.tensor.matmul(qkv_ps[:, n, :],
                                                    wqkv16[:, w, i, n * D:(n + 1) * D],
                                                    xnT[:, a, i, bass.ds(c * CHUNK, CHUNK)],
                                                    start=(i == 0 and (w, a) == (0, 0)),
                                                    stop=(i == HT - 1 and (w, a) == (1, 0)))
                    last.then_inc(s[name], 1)
                if not (isinstance(c, int) and c == 0):
                    pe.wait_ge(s["qkv_hi_ready"], c * 3)
                for t in range(TPC):
                    for i in range(HT):
                        for a, w in PAIRS:
                            last = nc.tensor.matmul(qkv_ps[:, 2, t * D:(t + 1) * D],
                                                    xnT[:, a, i, bass.ds(c * CHUNK + t * P, P)],
                                                    wqkv16[:, w, i, 2 * D:3 * D],
                                                    start=(i == 0 and (a, w) == (0, 0)),
                                                    stop=(i == HT - 1 and (a, w) == (1, 0)))
                last.then_inc(s["v_product"], 1)

            pe.wait_ge(s["identity_ready"], 1)
            transpose_xn(0)
            pe.wait_ge(s["w16_ready"], 2)
            pe.wait_ge(s["scales_ready"], 1)
            project(0)
            transpose_xn(1)
            with pe.Fori(1, NC - 1) as c:
                project(c)
                transpose_xn(c + 1)
            project(NC - 1)

            pe.wait_ge(s["consts_ready"], 1)
            pe.wait_ge(s["qkv_lo_ready"], 3 * NC)

            def max_scores(n, k):
                if not (isinstance(n, int) and n == 0 and k < 2):
                    pe.wait_ge(s["max_reduced"], n * RT + k - 1)
                nc.tensor.matmul(max_ps[:, k % 2, :], q16[:, 0, bass.ds(n * CHUNK + (k // 4) * P, P)],
                                 k16[:, 0, (k % 4) * CHUNK:(k % 4 + 1) * CHUNK],
                                 start=True, stop=True).then_inc(s["max_product"], 1)

            def scores(n, k):
                first = isinstance(n, int) and n == 0
                if not first or k >= 4:
                    pe.wait_ge(s["exp16_done"], n * RT + k - 3)
                for i, (a, b) in enumerate(PAIRS):
                    nc.tensor.matmul(score_ps[:, k % 4, :], k16[:, a, k * P:(k + 1) * P],
                                     q16[:, b, bass.ds(n * CHUNK, CHUNK)], start=(i == 0), stop=False)
                if k == 0:
                    pe.wait_ge(s["shift_ready"], n + 1)
                nc.tensor.matmul(score_ps[:, k % 4, :], shift_up[:], neg_max[:],
                                 start=False, stop=True).then_inc(s["score_product"], 1)

            def weighted_values(n, k):
                pe.wait_ge(s["p_lo_ready"], n * RT + k + 1)
                if k == 0 and not (isinstance(n, int) and n == 0):
                    pe.wait_ge(s["o_copied"], n)
                for i, (a, b) in enumerate(PAIRS):
                    last = nc.tensor.matmul(o_ps[:], v16[:, a, k, :], p16[:, k % 4, b, :],
                                            start=(k == 0 and i == 0), stop=(k == RT - 1 and i == 2))
                last.then_inc(s["pv_product"], 1)

            def spread_sum(m):
                pe.wait_ge(s["sum_split"], m + 1)
                if not (isinstance(m, int) and m == 0):
                    pe.wait_ge(s["attn_stored"], m * HT)
                for part in range(2):
                    last = nc.tensor.matmul(tail_ps[:], ones16[:], p_sum16[:, part, :],
                                            start=(part == 0), stop=(part == 1))
                last.then_inc(s["sum_spread"], 1)

            def attention_out(m, j):
                if j == 0:
                    pe.wait_ge(s["o_lo_ready"], m + 1)
                else:
                    pe.wait_ge(s["attn_stored"], m * HT + j)
                for i, (a, b) in enumerate(PAIRS):
                    last = nc.tensor.matmul(tail_ps[:], wo16[:, a, j * P:(j + 1) * P], o16[:, b, :],
                                            start=(i == 0), stop=(i == 2))
                last.then_inc(s["attn_product"], 1)

            LAG = 3

            def attention(n, with_previous, with_next):
                for k in range(RT):
                    if k >= LAG:
                        weighted_values(n, k - LAG)
                    elif with_previous:
                        weighted_values(n - 1, RT + k - LAG)
                    scores(n, k)
                    if with_next:
                        max_scores(n + 1, k)
                    if with_previous:
                        if k == 4:
                            spread_sum(n - 1)
                        if 11 <= k < 11 + HT:
                            attention_out(n - 1, k - 11)

            for k in range(RT):
                max_scores(0, k)
            attention(0, False, True)
            with pe.Fori(1, NC - 1) as n:
                attention(n, True, True)
            attention(NC - 1, True, False)
            for k in range(RT - LAG, RT):
                weighted_values(NC - 1, k)
            spread_sum(NC - 1)
            for j in range(HT):
                attention_out(NC - 1, j)

            pe.wait_ge(s["attn_stored"], NC * HT)
            pe.wait_ge(s["int4_landed"], 3 * 16)

            def drained(t, order, at):
                item = order[at]
                if item in ACT_DRAINS:
                    own = [x for x in ACT_DRAINS if x in order].index(item)
                    pe.wait_ge(s["act_drained"], act_drains_before(t) + own + 1)
                else:
                    own = [x for x in order if x in DVE_DRAINS].index(item)
                    pe.wait_ge(s["dve_drained"], dve_drains_before(t) + own + 1)

            def product(t, order, at, previous, h_parity, tile, y_tile, rows):
                if at >= RING:
                    drained(t, order, at - RING)
                elif previous is not None:
                    drained(t - 1, previous, len(previous) + at - RING)
                kind, g = order[at]
                for half in range(2):
                    dst = ffn_ps[:, at % RING, half, :]
                    for part in range(2):
                        if kind == "y":
                            last = nc.tensor.matmul(
                                dst, down16[:, bass.ds(y_tile, 1), g * P:(g + 1) * P].rearrange(
                                    "p a b -> p (a b)"),
                                h16[:, h_parity, part, half * CHUNK:(half + 1) * CHUNK],
                                start=(part == 0), stop=(part == 1))
                        else:
                            w16 = gate16 if kind == "g" else up16
                            r0 = rows + half * CHUNK
                            last = nc.tensor.matmul(dst, w16[:, g, bass.ds(tile * P, P)],
                                                    xnT[:, part, g, r0:r0 + CHUNK],
                                                    start=(part == 0), stop=(part == 1))
                last.then_inc(s["ffn_product"], 1)

            def ffn_step(t, parity, tile, y_tile, rows, previous):
                order = OPEN if y_tile is None else FULL
                for at in range(len(order)):
                    if order[at] == ("y", 0):
                        pe.wait_ge(s["h_lo_ready"], t - 1)
                    product(t, order, at, previous, parity, tile, y_tile, rows)

            ffn_step(0, 0, 0, None, 0, None)
            ffn_step(1, 1, 1, None, 0, OPEN)
            for half in range(NH):
                h2 = OT // 2
                rows = half * HALF
                if half == 0:
                    ffn_step(2, 0, 2, 0, rows, OPEN)
                    ffn_step(3, 1, 3, 1, rows, FULL)
                    first_pair = 2
                else:
                    ffn_step(half * OT, 0, 0, OT - 2, rows, FULL)
                    ffn_step(half * OT + 1, 1, 1, OT - 1, rows, FULL)
                    first_pair = half * h2 + 1
                with pe.Fori(first_pair, (half + 1) * h2) as pair:
                    ffn_step(pair * 2, 0, pair * 2 - half * OT, pair * 2 - half * OT - 2, rows, FULL)
                    ffn_step(pair * 2 + 1, 1, pair * 2 - half * OT + 1, pair * 2 - half * OT - 1,
                             rows, FULL)
            for t in (STEPS, STEPS + 1):
                pe.wait_ge(s["h_lo_ready"], t - 1)
                for j in range(HT):
                    if t == STEPS:
                        drained(STEPS - 1, FULL, len(FULL) + j - RING)
                    elif j == 0:
                        pe.wait_ge(s["dve_drained"], dve_drains_before(STEPS) + 1)
                    else:
                        pe.wait_ge(s["act_drained"], act_drains_before(STEPS) + j)
                    for half in range(2):
                        for part in range(2):
                            last = nc.tensor.matmul(
                                ffn_ps[:, j, half, :], down16[:, OT - 2 + t - STEPS, j * P:(j + 1) * P],
                                h16[:, t % 2, part, half * CHUNK:(half + 1) * CHUNK],
                                start=(part == 0), stop=(part == 1))
                    last.then_inc(s["ffn_product"], 1)


def kernel(L0_attn_x, L0_attn_Wqkv, L0_attn_bqkv, L0_attn_Wo, L0_attn_bo, L0_ffn_gate_q,
           L0_ffn_gate_s, L0_ffn_up_q, L0_ffn_up_s, L0_ffn_down_q, L0_ffn_down_s):
    import numpy as np
    import concourse.bacc as bacc
    from concourse.bass_utils import run_bass_kernel_spmd

    def columns(a, width):
        a = np.asarray(a).reshape(-1, P, width)
        return a.transpose(1, 0, 2)

    def grouped(q):
        q = np.asarray(q)
        return q.T.reshape(-1, P, q.shape[0]).transpose(1, 0, 2)

    x = np.asarray(L0_attn_x)[0]
    arrays = {
        "x": x, "xT": x.T, "wqkv": L0_attn_Wqkv,
        "bqkv": columns(L0_attn_bqkv, 1)[:, :, 0], "wo": L0_attn_Wo,
        "bo": columns(L0_attn_bo, 1)[:, :, 0],
        "gate_q": grouped(L0_ffn_gate_q), "gate_s": columns(L0_ffn_gate_s, HT),
        "up_q": grouped(L0_ffn_up_q), "up_s": columns(L0_ffn_up_s, HT),
        "down_q": grouped(L0_ffn_down_q), "down_s": columns(L0_ffn_down_s, OT),
    }
    arrays = {name: np.ascontiguousarray(a) for name, a in arrays.items()}
    nc = bacc.Bacc("TRN2", target_bir_lowering=False, num_devices=1)
    args = [nc.dram_tensor(name, a.shape, mybir.dt.from_np(a.dtype), kind="ExternalInput").ap()
            for name, a in arrays.items()]
    out = nc.dram_tensor("outT", (HID, ROWS), F32, kind="ExternalOutput").ap()
    build(nc, *args, out)
    result = run_bass_kernel_spmd(nc, [arrays], core_ids=[0])
    return np.asarray(result.results[0]["outT"]).T[None]
```

```python
from contextlib import ExitStack

import concourse.bass as bass
from concourse import mybir

F32 = mybir.dt.float32
F16 = mybir.dt.float16
BF16 = mybir.dt.bfloat16
I32 = mybir.dt.int32
ALU = mybir.AluOpType
ACT = mybir.ActivationFunctionType
AX_X = mybir.AxisListType.X
AX_XY = mybir.AxisListType.XY
ABSMAX = bass.bass_isa.ReduceOp.absmax

P = 128
ROWS = 2048
HID = 512
D = HID // 4
INNER = 1792
LN_EPS = 1e-5

HT = HID // P
OT = INNER // P
RT = ROWS // P
CHUNK = 512
NC = ROWS // CHUNK
TPC = CHUNK // P
HALF = 1024
NH = ROWS // HALF

X_EXP = 11
X_SCALE = float(2 ** X_EXP)
PROB_EXP = 8
SHIFT_EXP = 22
LN2 = 0.6931471805599453
QKV_L1 = 512.0
FFN_L1 = 4096.0
SCALE_BITS = float((127 + 14 + 127) << 23)
INVERSE_BITS = float((127 + 127) << 23)

FULL = [("g", 0), ("u", 0), ("y", 0), ("g", 1), ("u", 1), ("y", 1),
        ("g", 2), ("u", 2), ("y", 2), ("g", 3), ("u", 3), ("y", 3)]
OPEN = [x for x in FULL if x[0] != "y"]
ACT_DRAINS = [("g", 0), ("u", 0), ("y", 1), ("y", 2), ("y", 3)]
DVE_DRAINS = [x for x in FULL if x not in ACT_DRAINS]
RING = 4
STEPS = NH * OT

MAX_ITEMS = [2, 1, 1, 2, 1, 0, 1, 1, 1, 1, 1, 2, 1, 1, 0, 0]
SHIFT_AT = 13
INVERT_AT = 4
OUT_AT = 12
LAG = 3


def before(step, of, opening):
    if isinstance(step, int) and step <= 2:
        return opening * step
    return (step - 2) * of + 2 * opening


def slot_of(step, at):
    if isinstance(step, int) and step < 2:
        return (step * len(OPEN) + at + 2) % (RING - 1)
    return at % RING


def products_before(step):
    return before(step, len(FULL), len(OPEN))


def act_drains_before(step):
    return before(step, len(ACT_DRAINS), 2)


def dve_drains_before(step):
    return before(step, len(DVE_DRAINS), 6)


def build(nc, x, xT, wqkv, bqkv, wo, bo, gate_q, gate_s, up_q, up_s, down_q, down_s, outT):
    ctx = ExitStack()
    with ctx:
        def sb(name, shape, dt, scope=ctx):
            return scope.enter_context(nc.sbuf_tensor(name, shape, dt))

        def pb(name, shape, dt, scope=ctx):
            return scope.enter_context(nc.psum_tensor(name, shape, dt))

        def sem(name):
            return ctx.enter_context(nc.semaphore(name))

        gate16 = sb("gate16", [P, HT, INNER], F16)
        up16 = sb("up16", [P, HT, INNER], F16)
        down16 = sb("down16", [P, OT, HID], F16)
        xnT = sb("xnT", [P, 2, HT, ROWS], F16)
        attnT = sb("attnT", [P, HT, ROWS], F32)
        gate_col = sb("gate_col", [P, OT, HT], F32)
        up_col = sb("up_col", [P, OT, HT], F32)
        down_col = sb("down_col", [P, HT, OT], F32)
        gate_dq = sb("gate_dq", [P, OT, HT], F32)
        up_dq = sb("up_dq", [P, OT, HT], F32)
        down_dq = sb("down_dq", [P, HT, OT], F32)
        bo_col = sb("bo_col", [P, HT], F32)
        bqkv_col = sb("bqkv_col", [P, 3], F32)
        bqkv_sc = sb("bqkv_sc", [P, 3], F32)
        ident = sb("ident", [P, P], F16)
        ones16 = sb("ones16", [P, P], F16)
        shift_up = sb("shift_up", [P, P], BF16)
        shift_less = sb("shift_less", [P, 1], F32)
        max_less = sb("max_less", [P, TPC], F32)
        absmax = sb("absmax", [P, 5], F32)
        absmax_all = sb("absmax_all", [P, 5], F32)
        bound = sb("bound", [P, 4], F32)
        fit = sb("fit", [P, 4], F32)
        unfit = sb("unfit", [P, 4], F32)
        qkv_unscale = sb("qkv_unscale", [P, 1], F32)
        exp_scale = sb("exp_scale", [P, 1], F32)
        attn_unscale = sb("attn_unscale", [P, 1], F32)

        rows_scope = ExitStack()
        x_rows = sb("x_rows", [P, RT, HID], F32, rows_scope)
        rows_scope.close()
        ysum = sb("ysum", [P, HT, ROWS], F32)

        att = ExitStack()
        q16 = sb("q16", [P, 2, ROWS], F16, att)
        k16 = sb("k16", [P, 2, ROWS], F16, att)
        v16 = sb("v16", [P, 2, RT, D], F16, att)
        late = ExitStack()
        p32 = sb("p32", [P, 4, CHUNK], F32, late)
        p16 = sb("p16", [P, 4, 2, CHUNK], F16, late)
        wo16 = sb("wo16", [P, 2, HID], F16, late)
        max_parts = sb("max_parts", [P, TPC, 4], F32, late)
        max_col = sb("max_col", [P, TPC], F32, late)
        tail = ExitStack()
        p_sum = sb("p_sum", [P, CHUNK], F32, tail)
        p_sum16 = sb("p_sum16", [P, 2, CHUNK], F16, tail)
        neg_max = sb("neg_max", [P, NC, CHUNK], F16, tail)
        o_raw = sb("o_raw", [P, CHUNK], F32, tail)
        o_norm = sb("o_norm", [P, CHUNK], F32, tail)
        o32 = sb("o32", [P, CHUNK], F32, tail)
        o16 = sb("o16", [P, 2, CHUNK], F16, tail)
        inv_sum = sb("inv_sum", [P, CHUNK], F32, tail)
        tail.close()
        late.close()
        early = ExitStack()
        xn16 = sb("xn16", [P, 2 * TPC, 2, HID], F16, early)
        kept = ExitStack()
        sb("over_wo16_max", [P, 1024 + 64], F16, kept)
        wqkv16 = sb("wqkv16", [P, 2, HT, 3 * D], F16, kept)
        wqkv32 = sb("wqkv32", [P, HT, 3 * D], F32, kept)
        wo32 = sb("wo32", [P, HID], F32, kept)
        qkv32 = sb("qkv32", [P, 3, CHUNK], F32, kept)
        bn6 = sb("bn6", [P, RT, 6], F32, kept)
        mean_var = sb("mean_var", [P, RT, 2], F32, kept)
        var_eps = sb("var_eps", [P, RT], F32, kept)
        std = sb("std", [P, RT], F32, kept)
        rstd0 = sb("rstd0", [P, RT], F32, kept)
        newton = sb("newton", [P, RT], F32, kept)
        newton2 = sb("newton2", [P, RT], F32, kept)
        newton3 = sb("newton3", [P, RT], F32, kept)
        x_mul = sb("x_mul", [P, RT], F32, kept)
        x_add = sb("x_add", [P, RT], F32, kept)
        kept.close()
        early.close()
        att.close()

        ffn = ExitStack()
        g32 = sb("g32", [P, 2, HALF], F32, ffn)
        u32 = sb("u32", [P, 2, HALF], F32, ffn)
        silu32 = sb("silu32", [P, HALF], F32, ffn)
        h32 = sb("h32", [P, 2, HALF], F32, ffn)
        h16 = sb("h16", [P, 2, 2, HALF], F16, ffn)
        x_res = sb("x_res", [P, HT, HALF], F32, ffn)
        y_part = sb("y_part", [P, 3, HALF], F32, ffn)
        ffn.close()

        front = ExitStack()
        xn_ps = pb("xn_ps", [P, 2, 2, HT, P], F16, front)
        qkv_ps = pb("qkv_ps", [P, 3, CHUNK], F32, front)
        front.close()
        attps = ExitStack()
        score_ps = pb("score_ps", [P, 4, CHUNK], F32, attps)
        o_ps = pb("o_ps", [P, CHUNK], F32, attps)
        max_ps = pb("max_ps", [P, 2, CHUNK], F32, attps)
        tail_ps = pb("tail_ps", [P, CHUNK], F32, attps)
        attps.close()
        ffn_ps = pb("ffn_ps", [P, RING, 2, CHUNK], F32)

        names = """weights_landed wo_landed scales_landed residual_landed int4_landed
            out_stored identity_zeroed identity_ready consts_ready absmax_ready absmax_spread
            scales_ready fit_ready first_hi_ready first_ready xn32_done w16_hi w16_ready wo16_hi
            stats_ready var_ready std_ready moments_done moments_ready xn32_ready xn_hi_ready xn_lo_ready
            xn_transposed xn_stored q_product k_product v_product qkv32_ready qkv_hi_ready
            qkv_lo_ready max_product max_reduced max_done max_moved shift_ready score_product
            exp32_done exp16_done p_lo_ready pv_product p_summed sum_hi_ready sum_split sum_spread
            sum_inverted o_copied o_scaled o32_ready o_hi_ready o_lo_ready attn_product attn_stored
            dve_small ysum_zeroed ffn_product act_drained dve_drained silu_done h_ready h_hi_ready
            h_lo_ready y_added final_silu final_scaled final_ready""".split()
        s = {n: sem(n) for n in names}
        x_landed = [sem(f"x_landed_{c}") for c in range(NC)]

        def first(n):
            return isinstance(n, int) and n == 0

        block = ctx.enter_context(nc.Block())

        @block.sync
        def _(sp):
            xv = x.rearrange("(t p) h -> p t h", p=P)
            for c in range(NC):
                if c == 1:
                    sp.wait_ge(s["weights_landed"], 16)
                    sp.wait_ge(s["wo_landed"], 16)
                if c:
                    sp.wait_ge(x_landed[c - 1], 16)
                sp.dma_start(x_rows[:, c * TPC:(c + 1) * TPC, :],
                             xv[:, c * TPC:(c + 1) * TPC, :]).then_inc(x_landed[c], 16)
            xTv = xT.rearrange("(j p) r -> p j r", p=P)
            outv = outT.rearrange("(j p) r -> p j r", p=P)
            sp.wait_ge(s["attn_stored"], NC * HT)
            for half in range(NH):
                rows = slice(half * HALF, (half + 1) * HALF)
                if half:
                    sp.wait_ge(s["out_stored"], 16 * half * HT)
                sp.dma_start(x_res[:], xTv[:, :, rows]).then_inc(s["residual_landed"], 16)
                for j in range(HT):
                    sp.wait_ge(s["final_ready"], half * HT + j + 1)
                    sp.dma_start(outv[:, j, rows], x_res[:, j, :]).then_inc(s["out_stored"], 16)
            sp.wait_ge(s["out_stored"], 16 * NH * HT)

        @block.gpsimd
        def _(pool):
            nc.gpsimd.memset(ident[:], 0.0).then_inc(s["identity_zeroed"], 1)
            nc.gpsimd.memset(ones16[:], 1.0)
            nc.gpsimd.memset(shift_up[:], float(2 ** SHIFT_EXP)).then_inc(s["consts_ready"], 1)
            pool.wait_ge(s["identity_zeroed"], 1)
            nc.gpsimd.affine_select(out=ident[:], in_=ident[:], compare_op=ALU.not_equal, fill=1.0,
                                    base=0, pattern=[[-1, P]], channel_multiplier=1
                                    ).then_inc(s["identity_ready"], 1)
            pool.wait_ge(s["absmax_ready"], 1)
            nc.gpsimd.partition_all_reduce(absmax_all[:], absmax[:], P, ABSMAX
                                           ).then_inc(s["absmax_spread"], 1)

            for t in range(1, RT):
                if t % TPC == 0 or t == 1:
                    pool.wait_ge(s["moments_ready"], t // TPC + 1)
                if t >= 2 * TPC:
                    pool.wait_ge(s["xn_transposed"], t - 2 * TPC + 1)
                nc.gpsimd.tensor_scalar(xn16[:, t % (2 * TPC), 0, :], x_rows[:, t, :],
                                        x_mul[:, t:t + 1], x_add[:, t:t + 1],
                                        ALU.mult, ALU.add).then_inc(s["xn_hi_ready"], 1)
                if t < 2 * TPC:
                    continue
                pool.wait_ge(s["xn_hi_ready"], t)
                nc.gpsimd.tensor_scalar(x_rows[:, t, :], x_rows[:, t, :],
                                        x_mul[:, t:t + 1], x_add[:, t:t + 1],
                                        ALU.mult, ALU.add).then_inc(s["xn32_ready"], 1)
            for dst, src in ((gate16, gate_q), (up16, up_q), (down16, down_q)):
                pool.dma_start(dst[:], src).then_inc(s["int4_landed"], 16)
            pool.wait_ge(s["xn_lo_ready"], RT)
            nc.gpsimd.memset(ysum[:], 0.0).then_inc(s["ysum_zeroed"], 1)

            def sum_probabilities(n):
                for k in range(1, RT):
                    pool.wait_ge(s["exp32_done"], n * RT + k + 1)
                    if k == 1:
                        if not first(n):
                            pool.wait_ge(s["sum_split"], n)
                        total = p32[:, 0, :]
                    else:
                        pool.wait_ge(s["p_summed"], n * (RT - 1) + k - 1)
                        total = p_sum[:]
                    nc.gpsimd.tensor_tensor(p_sum[:], total, p32[:, k % 4, :], ALU.add
                                            ).then_inc(s["p_summed"], 1)

            sum_probabilities(0)
            with pool.Fori(1, NC) as n:
                sum_probabilities(n)

            def add(t, j, rows, drained):
                pool.wait_ge(s["act_drained"], drained)
                if not (isinstance(t, int) and t == 2):
                    pool.wait_ge(s["y_added"], (t - 3) * 3 + j)
                nc.gpsimd.tensor_tensor(ysum[:, j, rows], ysum[:, j, rows], y_part[:, j - 1, :],
                                        ALU.add).then_inc(s["y_added"], 1)

            def ffn_step(t, parity, half):
                with_y = half is not None
                if with_y:
                    rows = slice(half * HALF, (half + 1) * HALF)
                    add(t, 1, rows, act_drains_before(t) + 3)
                pool.wait_ge(s["h_hi_ready"], t)
                nc.gpsimd.tensor_tensor(h16[:, parity, 1, :], h32[:, parity, :],
                                        h16[:, parity, 0, :], ALU.subtract).then_inc(s["h_lo_ready"], 1)
                if with_y:
                    add(t, 2, rows, act_drains_before(t) + 4)
                    add(t, 3, rows, act_drains_before(t) + 5)

            def final_add(half, j):
                rows = slice(half * HALF, (half + 1) * HALF)
                pool.wait_ge(s["final_scaled"], half * HT + j + 1)
                pool.wait_ge(s["residual_landed"], 16 * (half + 1))
                xr = x_res[:, j, :] if isinstance(j, int) else \
                    x_res[:, bass.ds(j, 1), :].rearrange("p a r -> p (a r)")
                ys = ysum[:, j, rows] if isinstance(j, int) else \
                    ysum[:, bass.ds(j, 1), rows].rearrange("p a r -> p (a r)")
                nc.gpsimd.tensor_tensor(xr, ys, xr, ALU.add).then_inc(s["final_ready"], 1)

            ffn_step(1, 0, None)
            ffn_step(2, 1, 0)
            ffn_step(3, 0, 0)
            with pool.Fori(2, OT // 2) as pair:
                ffn_step(pair * 2, 1, 0)
                ffn_step(pair * 2 + 1, 0, 0)
            ffn_step(OT, 1, 0)
            ffn_step(OT + 1, 0, 0)
            with pool.Fori(0, HT) as j:
                ffn_step(j * 2 + OT + 2, 1, 1)
                ffn_step(j * 2 + OT + 3, 0, 1)
                final_add(0, j)
            with pool.Fori(OT // 2 + 1 + HT, OT) as pair:
                ffn_step(pair * 2, 1, 1)
                ffn_step(pair * 2 + 1, 0, 1)
            rows = slice((NH - 1) * HALF, NH * HALF)
            add(STEPS, 2, rows, act_drains_before(STEPS) + 1)
            add(STEPS, 3, rows, act_drains_before(STEPS) + 2)
            final_add(NH - 1, 0)
            final_add(NH - 1, 1)

        @block.scalar
        def _(act):
            act.dma_start(wqkv32[:], wqkv.rearrange("(i p) f -> p i f", p=P)
                          ).then_inc(s["weights_landed"], 16)
            act.dma_start(bqkv_col[:], bqkv).then_inc(s["scales_landed"], 16)
            act.dma_start(gate_col[:], gate_s).then_inc(s["scales_landed"], 16)
            act.dma_start(up_col[:], up_s).then_inc(s["scales_landed"], 16)
            act.dma_start(wo32[:], wo).then_inc(s["wo_landed"], 16)
            act.dma_start(bo_col[:], bo).then_inc(s["scales_landed"], 16)
            act.dma_start(down_col[:], down_s).then_inc(s["scales_landed"], 16)

            def square_root(c):
                tiles = slice(c * TPC, (c + 1) * TPC)
                act.wait_ge(s["var_ready"], c + 1)
                nc.scalar.activation(std[:, tiles], var_eps[:, tiles], ACT.Sqrt
                                     ).then_inc(s["std_ready"], 1)

            def store_transposed(c, tiles):
                for t in tiles:
                    act.wait_ge(s["xn_transposed"], c * TPC + t + 1)
                    nc.scalar.activation(xnT[:, :, :, bass.ds(c * CHUNK + t * P, P)],
                                         xn_ps[:, t % 2, :, :, :], ACT.Copy
                                         ).then_inc(s["xn_stored"], 1)

            def store_qk(c):
                for i, (product, dst) in enumerate((("q_product", q16), ("k_product", k16))):
                    act.wait_ge(s[product], c + 1)
                    if not first(c):
                        act.wait_ge(s["qkv_lo_ready"], c * 3 - 2 + i)
                    args = dict(scale=qkv_unscale[:, 0:1], bias=bqkv_sc[:, i:i + 1])
                    nc.scalar.activation(dst[:, 0, bass.ds(c * CHUNK, CHUNK)], qkv_ps[:, i, :],
                                         ACT.Identity, **args).then_inc(s["qkv_hi_ready"], 1)
                    nc.scalar.activation(qkv32[:, i, :], qkv_ps[:, i, :], ACT.Identity, **args
                                         ).then_inc(s["qkv32_ready"], 1)

            def store_v(c):
                act.wait_ge(s["v_product"], c + 1)
                if not first(c):
                    act.wait_ge(s["qkv_lo_ready"], c * 3)
                nc.scalar.activation(v16[:, 0, bass.ds(c * TPC, TPC), :],
                                     qkv_ps[:, 2, :].rearrange("p (t d) -> p t d", d=D), ACT.Copy,
                                     scale=qkv_unscale[:, 0:1]).then_inc(s["qkv_hi_ready"], 1)
                nc.scalar.activation(qkv32[:, 2, :], qkv_ps[:, 2, :], ACT.Copy,
                                     scale=qkv_unscale[:, 0:1]).then_inc(s["qkv32_ready"], 1)

            square_root(0)
            act.wait_ge(s["moments_ready"], 1)
            nc.scalar.activation(xn16[:, 0, 0, :], x_rows[:, 0, :], ACT.Identity,
                                 scale=x_mul[:, 0:1], bias=x_add[:, 0:1]
                                 ).then_inc(s["first_hi_ready"], 1)
            act.wait_ge(s["first_hi_ready"], 1)
            nc.scalar.activation(x_rows[:, 0, :], x_rows[:, 0, :], ACT.Identity,
                                 scale=x_mul[:, 0:1], bias=x_add[:, 0:1]
                                 ).then_inc(s["first_ready"], 1)
            act.wait_ge(s["fit_ready"], 1)
            nc.scalar.activation(wqkv16[:, 0, :, :], wqkv32[:], ACT.Copy, scale=fit[:, 0:1]
                                 ).then_inc(s["w16_hi"], 1)
            store_transposed(0, range(TPC))
            nc.scalar.activation(wo16[:, 0, :], wo32[:], ACT.Copy, scale=fit[:, 1:2]
                                 ).then_inc(s["wo16_hi"], 1)
            square_root(1)
            for c in range(NC):
                store_qk(c)
                if c == 0:
                    store_v(0)
                    store_transposed(1, (0, 1))
                    square_root(2)
                    store_transposed(1, (2, 3))
                    square_root(3)
                    continue
                if c + 1 < NC:
                    store_transposed(c + 1, range(TPC))
                store_v(c)

            def exponentials(n, k):
                act.wait_ge(s["score_product"], n * RT + k + 1)
                if not first(n) or k >= 4:
                    act.wait_ge(s["p_lo_ready"], n * RT + k - 3)
                    if k >= 4:
                        act.wait_ge(s["p_summed"], n * (RT - 1) + max(k - 4, 1))
                    else:
                        act.wait_ge(s["p_summed"], n * (RT - 1) + k - 3)
                    act.wait_ge(s["pv_product"], n * RT + k - 3)
                nc.scalar.activation(p32[:, k % 4, :], score_ps[:, k % 4, :], ACT.Exp,
                                     scale=exp_scale[:, 0:1]).then_inc(s["exp32_done"], 1)
                nc.scalar.activation(p16[:, k % 4, 0, :], score_ps[:, k % 4, :], ACT.Exp,
                                     scale=exp_scale[:, 0:1]).then_inc(s["exp16_done"], 1)

            def copy_o(m):
                act.wait_ge(s["pv_product"], (m + 1) * RT)
                if not first(m):
                    act.wait_ge(s["o_scaled"], m)
                nc.scalar.activation(o_raw[:], o_ps[:], ACT.Copy).then_inc(s["o_copied"], 1)

            def add_v_bias(m):
                act.wait_ge(s["o_scaled"], m + 1)
                if not first(m):
                    act.wait_ge(s["o_lo_ready"], m)
                    act.wait_ge(s["attn_product"], m * HT)
                args = dict(bias=bqkv_sc[:, 2:3])
                nc.scalar.activation(o32[:], o_norm[:], ACT.Identity, **args).then_inc(s["o32_ready"], 1)
                nc.scalar.activation(o16[:, 0, :], o_norm[:], ACT.Identity, **args
                                     ).then_inc(s["o_hi_ready"], 1)

            def store_attention(m, j):
                act.wait_ge(s["attn_product"], m * HT + j + 1)
                nc.scalar.activation(attnT[:, j, bass.ds(m * CHUNK, CHUNK)], tail_ps[:], ACT.Identity,
                                     scale=attn_unscale[:, 0:1], bias=bo_col[:, j:j + 1]
                                     ).then_inc(s["attn_stored"], 1)

            def attention(n, with_tail):
                for k in range(RT):
                    exponentials(n, k)
                    if with_tail:
                        if k == 1:
                            copy_o(n - 1)
                        if k == INVERT_AT + TPC + 1:
                            add_v_bias(n - 1)
                        if k >= OUT_AT:
                            store_attention(n - 1, k - OUT_AT)

            act.wait_ge(s["xn_transposed"], RT)
            attention(0, False)
            with act.Fori(1, NC) as n:
                attention(n, True)

            def drain(t, order, item, dst, scale):
                act.wait_ge(s["ffn_product"], products_before(t) + order.index(item) + 1)
                src = ffn_ps[:, slot_of(t, order.index(item)), :, :]
                nc.scalar.activation(dst.rearrange("p (a b) -> p a b", b=CHUNK), src, ACT.Copy,
                                     scale=scale).then_inc(s["act_drained"], 1)

            def start_sums(t, order, parity, tile):
                if not (isinstance(t, int) and t < 2):
                    act.wait_ge(s["h_ready"], t - 1)
                drain(t, order, ("g", 0), g32[:, parity, :], gate_dq[:, bass.ds(tile, 1), 0])
                drain(t, order, ("u", 0), u32[:, parity, :], up_dq[:, bass.ds(tile, 1), 0])

            def silu_of(t, parity):
                act.wait_ge(s["dve_drained"], dve_drains_before(t + 1) - 1)
                if not first(t):
                    act.wait_ge(s["h_ready"], t)
                nc.scalar.activation(silu32[:], g32[:, parity, :], ACT.Silu).then_inc(s["silu_done"], 1)

            def h_hi(t, parity):
                act.wait_ge(s["h_ready"], t + 1)
                if not (isinstance(t, int) and t < 2):
                    act.wait_ge(s["ffn_product"], products_before(t + 1))
                nc.scalar.activation(h16[:, parity, 0, :], h32[:, parity, :], ACT.Copy
                                     ).then_inc(s["h_hi_ready"], 1)

            def y_drain(t, order, tile, j):
                if not (isinstance(t, int) and t == 2):
                    act.wait_ge(s["y_added"], (t - 3) * 3 + j)
                drain(t, order, ("y", j), y_part[:, j - 1, :], down_dq[:, j, bass.ds(tile, 1)])

            def ffn_step(t, parity, tile, y_tile):
                start_sums(t, FULL, parity, tile)
                y_drain(t, FULL, y_tile, 1)
                h_hi(t - 1, 1 - parity)
                y_drain(t, FULL, y_tile, 2)
                silu_of(t, parity)
                y_drain(t, FULL, y_tile, 3)

            def final_silu(half, j):
                rows = slice(half * HALF, (half + 1) * HALF)
                nc.scalar.activation(ysum[:, bass.ds(j, 1), rows], ysum[:, bass.ds(j, 1), rows],
                                     ACT.Silu).then_inc(s["final_silu"], 1)

            copy_o(NC - 1)
            act.wait_ge(s["p_summed"], NC * (RT - 1))
            start_sums(0, OPEN, 0, 0)
            add_v_bias(NC - 1)
            silu_of(0, 0)
            start_sums(1, OPEN, 1, 1)
            for j in range(2):
                store_attention(NC - 1, j)
            h_hi(0, 0)
            for j in range(2, HT):
                store_attention(NC - 1, j)
            silu_of(1, 1)
            ffn_step(2, 0, 2, 0)
            ffn_step(3, 1, 3, 1)
            with act.Fori(2, OT // 2) as pair:
                ffn_step(pair * 2, 0, pair * 2, pair * 2 - 2)
                ffn_step(pair * 2 + 1, 1, pair * 2 + 1, pair * 2 - 1)
            ffn_step(OT, 0, 0, OT - 2)
            ffn_step(OT + 1, 1, 1, OT - 1)
            with act.Fori(0, HT) as j:
                act.wait_ge(s["y_added"], 3 * OT)
                act.wait_ge(s["dve_drained"], dve_drains_before(OT + 1) + 1)
                final_silu(0, j)
                ffn_step(j * 2 + OT + 2, 0, j * 2 + 2, j * 2)
                ffn_step(j * 2 + OT + 3, 1, j * 2 + 3, j * 2 + 1)
            with act.Fori(OT // 2 + 1 + HT, OT) as pair:
                ffn_step(pair * 2, 0, pair * 2 - OT, pair * 2 - OT - 2)
                ffn_step(pair * 2 + 1, 1, pair * 2 + 1 - OT, pair * 2 - OT - 1)
            h_hi(STEPS - 1, 1)
            for i, j in enumerate((2, 3)):
                act.wait_ge(s["y_added"], (STEPS - 3) * 3 + j)
                act.wait_ge(s["ffn_product"], products_before(STEPS) + i + 1)
                nc.scalar.activation(y_part[:, j - 1, :].rearrange("p (a b) -> p a b", b=CHUNK),
                                     ffn_ps[:, j, :, :], ACT.Copy, scale=down_dq[:, j, OT - 2:OT - 1]
                                     ).then_inc(s["act_drained"], 1)
            for j in range(HT):
                act.wait_ge(s["dve_drained"], dve_drains_before(STEPS) + 2 + j + 1)
                final_silu(NH - 1, j)

        @block.vector
        def _(dve):
            small = [0]

            def chain(op):
                small[0] += 1
                op.then_inc(s["dve_small"], 1)
                dve.wait_ge(s["dve_small"], small[0])

            def statistics(c):
                dve.wait_ge(x_landed[c], 16)
                for t in range(c * TPC, (c + 1) * TPC):
                    last = nc.vector.bn_stats(bn6[:, t, :], x_rows[:, t, :])
                last.then_inc(s["stats_ready"], 1)

            def variances(c):
                tiles = slice(c * TPC, (c + 1) * TPC)
                dve.wait_ge(s["stats_ready"], c + 1)
                for t in range(tiles.start, tiles.stop):
                    last = nc.vector.bn_aggr(mean_var[:, t, :], bn6[:, t, :])
                chain(last)
                nc.vector.tensor_scalar(var_eps[:, tiles], mean_var[:, tiles, 1], LN_EPS, None, ALU.add
                                        ).then_inc(s["var_ready"], 1)

            def factors(c):
                tiles = slice(c * TPC, (c + 1) * TPC)
                dve.wait_ge(s["std_ready"], c + 1)
                chain(nc.vector.reciprocal(rstd0[:, tiles], std[:, tiles]))
                chain(nc.vector.tensor_tensor(newton[:, tiles], var_eps[:, tiles], rstd0[:, tiles],
                                              ALU.mult))
                chain(nc.vector.tensor_tensor(newton2[:, tiles], newton[:, tiles], rstd0[:, tiles],
                                              ALU.mult))
                chain(nc.vector.tensor_scalar(newton3[:, tiles], newton2[:, tiles], -0.5 * X_SCALE,
                                              1.5 * X_SCALE, ALU.mult, ALU.add))
                chain(nc.vector.tensor_tensor(x_mul[:, tiles], newton3[:, tiles], rstd0[:, tiles],
                                              ALU.mult))
                op = nc.vector.scalar_tensor_tensor(x_add[:, tiles], mean_var[:, tiles, 0], -1.0,
                                                    x_mul[:, tiles], ALU.mult, ALU.mult)
                op.then_inc(s["moments_ready"], 1)

            def normalise(t):
                dve.wait_ge(s["moments_ready"], t // TPC + 1)
                dve.wait_ge(s["xn_hi_ready"], t)
                nc.vector.tensor_scalar(x_rows[:, t, :], x_rows[:, t, :], x_mul[:, t:t + 1],
                                        x_add[:, t:t + 1], ALU.mult, ALU.add
                                        ).then_inc(s["xn32_done"], 1)

            def split_xn(t):
                if t == 0:
                    dve.wait_ge(s["first_ready"], 1)
                elif t < 2 * TPC:
                    dve.wait_ge(s["xn32_done"], t)
                else:
                    dve.wait_ge(s["xn32_ready"], t - 2 * TPC + 1)
                slot = t % (2 * TPC)
                nc.vector.tensor_tensor(xn16[:, slot, 1, :], x_rows[:, t, :], xn16[:, slot, 0, :],
                                        ALU.subtract).then_inc(s["xn_lo_ready"], 1)

            def split_qk(c):
                for i, dst in enumerate((q16, k16)):
                    dve.wait_ge(s["qkv32_ready"], c * 3 + i + 1)
                    nc.vector.tensor_tensor(dst[:, 1, bass.ds(c * CHUNK, CHUNK)], qkv32[:, i, :],
                                            dst[:, 0, bass.ds(c * CHUNK, CHUNK)],
                                            ALU.subtract).then_inc(s["qkv_lo_ready"], 1)

            def split_v(c):
                dve.wait_ge(s["qkv32_ready"], c * 3 + 3)
                nc.vector.tensor_tensor(v16[:, 1, bass.ds(c * TPC, TPC), :],
                                        qkv32[:, 2, :].rearrange("p (t d) -> p t d", d=D),
                                        v16[:, 0, bass.ds(c * TPC, TPC), :],
                                        ALU.subtract).then_inc(s["qkv_lo_ready"], 1)

            def reduce_scores(n, item):
                dve.wait_ge(s["max_product"], n * RT + item + 1)
                nc.vector.reduce_max(max_parts[:, item % 4, item // 4:item // 4 + 1],
                                     max_ps[:, item % 2, :], AX_X).then_inc(s["max_reduced"], 1)

            statistics(0)
            variances(0)
            dve.wait_ge(s["weights_landed"], 16)
            nc.vector.reduce_max(absmax[:, 0:1], wqkv32[:], AX_XY, apply_absolute_value=True)
            dve.wait_ge(s["wo_landed"], 16)
            nc.vector.reduce_max(absmax[:, 1:2], wo32[:], AX_X, apply_absolute_value=True)
            dve.wait_ge(s["scales_landed"], 5 * 16)
            nc.vector.reduce_max(absmax[:, 2:3], bqkv_col[:], AX_X, apply_absolute_value=True)
            nc.vector.reduce_max(absmax[:, 3:4], gate_col[:], AX_XY, apply_absolute_value=True)
            nc.vector.reduce_max(absmax[:, 4:5], up_col[:], AX_XY, apply_absolute_value=True
                                 ).then_inc(s["absmax_ready"], 1)
            factors(0)
            dve.wait_ge(s["absmax_spread"], 1)
            nc.vector.tensor_scalar(bound[:, 0:2], absmax_all[:, 0:2], 2.0 ** -20, None, ALU.max)
            chain(nc.vector.scalar_tensor_tensor(bound[:, 2:3], absmax_all[:, 0:1], QKV_L1,
                                                 absmax_all[:, 2:3], ALU.mult, ALU.add))
            chain(nc.vector.tensor_scalar(bound[:, 3:4], absmax_all[:, 3:4], absmax_all[:, 4:5],
                                          FFN_L1 * FFN_L1, ALU.mult, ALU.mult))
            chain(nc.vector.tensor_scalar(bound[:, 2:4], bound[:, 2:4], 2.0 ** -20, None, ALU.max))
            chain(nc.vector.tensor_scalar(fit[:].bitcast(I32), bound[:].bitcast(I32), 0x7F800000, None,
                                          ALU.bitwise_and))
            nc.vector.tensor_scalar(fit[:].bitcast(I32), fit[:].bitcast(I32), -1.0, SCALE_BITS,
                                    ALU.mult, ALU.add).then_inc(s["fit_ready"], 1)
            dve.wait_ge(s["fit_ready"], 1)
            chain(nc.vector.tensor_scalar(unfit[:].bitcast(I32), fit[:].bitcast(I32), -1.0,
                                          INVERSE_BITS, ALU.mult, ALU.add))
            nc.vector.tensor_scalar(qkv_unscale[:], unfit[:, 0:1], fit[:, 2:3], 1.0 / X_SCALE,
                                    ALU.mult, ALU.mult)
            nc.vector.tensor_scalar(bqkv_sc[:], bqkv_col[:], fit[:, 2:3], None, ALU.mult)
            nc.vector.tensor_scalar(exp_scale[:], unfit[:, 2:3], unfit[:, 2:3], float(D) ** -0.5,
                                    ALU.mult, ALU.mult)
            nc.vector.tensor_scalar(shift_less[:], fit[:, 2:3], fit[:, 2:3],
                                    PROB_EXP * LN2 * float(D) ** 0.5, ALU.mult, ALU.mult)
            nc.vector.tensor_tensor(attn_unscale[:], unfit[:, 1:2], unfit[:, 2:3], ALU.mult)
            nc.vector.tensor_scalar(gate_dq[:], gate_col[:], 1.0 / X_SCALE, None, ALU.mult)
            nc.vector.tensor_scalar(up_dq[:], up_col[:], fit[:, 3:4], 1.0 / X_SCALE, ALU.mult, ALU.mult)
            nc.vector.tensor_scalar(down_dq[:], down_col[:], unfit[:, 3:4], None, ALU.mult
                                    ).then_inc(s["scales_ready"], 1)
            split_xn(0)
            for t in range(1, TPC):
                normalise(t)
            for t in range(1, TPC):
                split_xn(t)
            dve.wait_ge(s["w16_hi"], 1)
            nc.vector.scalar_tensor_tensor(wqkv16[:, 1, :, :], wqkv32[:], fit[:, 0:1],
                                           wqkv16[:, 0, :, :], ALU.mult, ALU.subtract
                                           ).then_inc(s["w16_ready"], 1)
            statistics(1)
            variances(1)
            dve.wait_ge(s["wo16_hi"], 1)
            nc.vector.scalar_tensor_tensor(wo16[:, 1, :], wo32[:], fit[:, 1:2], wo16[:, 0, :],
                                           ALU.mult, ALU.subtract).then_inc(s["w16_ready"], 1)
            factors(1)
            statistics(2)
            for t in range(TPC, 2 * TPC):
                normalise(t)
            for t in range(TPC, 2 * TPC):
                split_xn(t)
            variances(2)
            factors(2)
            split_qk(0)
            statistics(3)
            variances(3)
            factors(3)
            split_v(0)
            for c in range(1, NC):
                for pair in ((0, 1), (2, 3)):
                    for t in pair:
                        if c + 1 < NC:
                            split_xn((c + 1) * TPC + t)
                    for t in pair:
                        reduce_scores(0, (c - 1) * TPC + t)
                split_qk(c)
                if c + 1 < NC:
                    split_v(c)
            for t in range(TPC):
                reduce_scores(0, (NC - 1) * TPC + t)

            def shift_of(n):
                dve.wait_ge(s["max_reduced"], (n + 1) * RT)
                nc.vector.reduce_max(max_col[:], max_parts[:], AX_X).then_inc(s["max_done"], 1)
                dve.wait_ge(s["max_done"], n + 1)
                nc.vector.tensor_scalar(max_less[:], max_col[:], shift_less[:, 0:1],
                                        -(2.0 ** -SHIFT_EXP), ALU.subtract, ALU.mult
                                        ).then_inc(s["max_moved"], 1)
                dve.wait_ge(s["max_moved"], n + 1)
                for j in range(TPC):
                    block_of = neg_max[:, bass.ds(n, 1), j * P:(j + 1) * P].rearrange("p a q -> p (a q)")
                    last = nc.vector.tensor_scalar(block_of, ident[:], max_less[:, j:j + 1], None,
                                                   ALU.mult)
                last.then_inc(s["shift_ready"], 1)

            def p_lo(n, k):
                dve.wait_ge(s["exp16_done"], n * RT + k + 1)
                nc.vector.tensor_tensor(p16[:, k % 4, 1, :], p32[:, k % 4, :], p16[:, k % 4, 0, :],
                                        ALU.subtract).then_inc(s["p_lo_ready"], 1)

            def split_sum(m):
                dve.wait_ge(s["p_summed"], (m + 1) * (RT - 1))
                if not first(m):
                    dve.wait_ge(s["sum_spread"], m)
                nc.vector.tensor_copy(p_sum16[:, 0, :], p_sum[:]).then_inc(s["sum_hi_ready"], 1)
                dve.wait_ge(s["sum_hi_ready"], m + 1)
                nc.vector.tensor_tensor(p_sum16[:, 1, :], p_sum[:], p_sum16[:, 0, :], ALU.subtract
                                        ).then_inc(s["sum_split"], 1)

            def invert_sum(m, j):
                dve.wait_ge(s["sum_spread"], m + 1)
                part = slice(j * P, (j + 1) * P)
                nc.vector.reciprocal(inv_sum[:, part], tail_ps[:, part]).then_inc(s["sum_inverted"], 1)

            def scale_o(m):
                dve.wait_ge(s["o_copied"], m + 1)
                dve.wait_ge(s["sum_inverted"], (m + 1) * TPC)
                if not first(m):
                    dve.wait_ge(s["o_hi_ready"], m)
                nc.vector.tensor_tensor(o_norm[:], o_raw[:], inv_sum[:], ALU.mult
                                        ).then_inc(s["o_scaled"], 1)

            def split_o(m):
                dve.wait_ge(s["o_hi_ready"], m + 1)
                nc.vector.tensor_tensor(o16[:, 1, :], o32[:], o16[:, 0, :], ALU.subtract
                                        ).then_inc(s["o_lo_ready"], 1)

            def attention(n, with_tail, with_next):
                item = 0
                for k in range(RT):
                    if with_next:
                        for _ in range(MAX_ITEMS[k]):
                            reduce_scores(n + 1, item)
                            item += 1
                    p_lo(n, k)
                    if with_next and k == SHIFT_AT:
                        shift_of(n + 1)
                    if with_tail:
                        if k == 1:
                            split_sum(n - 1)
                        if INVERT_AT <= k < INVERT_AT + TPC:
                            invert_sum(n - 1, k - INVERT_AT)
                        if k == INVERT_AT + TPC:
                            scale_o(n - 1)
                        if k == INVERT_AT + TPC + 2:
                            split_o(n - 1)

            shift_of(0)
            split_v(NC - 1)
            attention(0, False, True)
            with dve.Fori(1, NC - 1) as n:
                attention(n, True, True)
            attention(NC - 1, True, False)

            def accumulate(t, order, item, dst, scale):
                dve.wait_ge(s["ffn_product"], products_before(t) + order.index(item) + 1)
                dst = dst.rearrange("p (a b) -> p a b", b=CHUNK)
                nc.vector.scalar_tensor_tensor(dst, ffn_ps[:, slot_of(t, order.index(item)), :, :], scale,
                                               dst, ALU.mult, ALU.add).then_inc(s["dve_drained"], 1)

            def make_h(t, parity):
                dve.wait_ge(s["silu_done"], t + 1)
                dve.wait_ge(s["dve_drained"], dve_drains_before(t + 1))
                if not (isinstance(t, int) and t < 2):
                    dve.wait_ge(s["h_lo_ready"], t - 1)
                nc.vector.tensor_tensor(h32[:, parity, :], silu32[:], u32[:, parity, :], ALU.mult
                                        ).then_inc(s["h_ready"], 1)

            def gate_up(t, order, parity, tile, g, done):
                if g == 1:
                    dve.wait_ge(s["act_drained"], act_drains_before(t) + 1)
                else:
                    dve.wait_ge(s["dve_drained"], done + 2 * g - 3)
                accumulate(t, order, ("g", g), g32[:, parity, :], gate_dq[:, bass.ds(tile, 1), g])
                if g == 1:
                    dve.wait_ge(s["act_drained"], act_drains_before(t) + 2)
                else:
                    dve.wait_ge(s["dve_drained"], done + 2 * g - 2)
                accumulate(t, order, ("u", g), u32[:, parity, :], up_dq[:, bass.ds(tile, 1), g])

            def ffn_step(t, parity, tile, y_tile, half):
                rows = slice(half * HALF, (half + 1) * HALF)
                if isinstance(t, int) and t == 2:
                    dve.wait_ge(s["ysum_zeroed"], 1)
                else:
                    dve.wait_ge(s["dve_drained"], dve_drains_before(t) - 6)
                accumulate(t, FULL, ("y", 0), ysum[:, 0, rows], down_dq[:, 0, bass.ds(y_tile, 1)])
                for g in range(1, HT):
                    gate_up(t, FULL, parity, tile, g, dve_drains_before(t) + 1)
                make_h(t, parity)

            def final_scale(half, j):
                rows = slice(half * HALF, (half + 1) * HALF)
                dve.wait_ge(s["final_silu"], half * HT + j + 1)
                ys = ysum[:, bass.ds(j, 1), rows]
                nc.vector.tensor_tensor(ys, ys, attnT[:, bass.ds(j, 1), rows], ALU.mult
                                        ).then_inc(s["final_scaled"], 1)

            split_sum(NC - 1)
            gate_up(0, OPEN, 0, 0, 1, 0)
            for j in range(TPC):
                invert_sum(NC - 1, j)
            scale_o(NC - 1)
            gate_up(0, OPEN, 0, 0, 2, 0)
            gate_up(0, OPEN, 0, 0, 3, 0)
            split_o(NC - 1)
            make_h(0, 0)
            for g in range(1, HT):
                gate_up(1, OPEN, 1, 1, g, dve_drains_before(1))
            make_h(1, 1)
            ffn_step(2, 0, 2, 0, 0)
            ffn_step(3, 1, 3, 1, 0)
            with dve.Fori(2, OT // 2) as pair:
                ffn_step(pair * 2, 0, pair * 2, pair * 2 - 2, 0)
                ffn_step(pair * 2 + 1, 1, pair * 2 + 1, pair * 2 - 1, 0)
            ffn_step(OT, 0, 0, OT - 2, 0)
            ffn_step(OT + 1, 1, 1, OT - 1, 0)
            with dve.Fori(0, HT) as j:
                ffn_step(j * 2 + OT + 2, 0, j * 2 + 2, j * 2, 1)
                final_scale(0, j)
                ffn_step(j * 2 + OT + 3, 1, j * 2 + 3, j * 2 + 1, 1)
            with dve.Fori(OT // 2 + 1 + HT, OT) as pair:
                ffn_step(pair * 2, 0, pair * 2 - OT, pair * 2 - OT - 2, 1)
                ffn_step(pair * 2 + 1, 1, pair * 2 + 1 - OT, pair * 2 - OT - 1, 1)
            rows = slice((NH - 1) * HALF, NH * HALF)

            def close(product, j, tile, sums):
                dve.wait_ge(s["ffn_product"], products_before(STEPS) + product + 1)
                dve.wait_ge(s[sums[0]], sums[1])
                dst = ysum[:, j, rows].rearrange("p (a b) -> p a b", b=CHUNK)
                nc.vector.scalar_tensor_tensor(dst, ffn_ps[:, j, :, :], down_dq[:, j, tile:tile + 1],
                                               dst, ALU.mult, ALU.add).then_inc(s["dve_drained"], 1)

            done = dve_drains_before(STEPS)
            close(2, 0, OT - 2, ("dve_drained", done - 6))
            close(3, 1, OT - 2, ("y_added", 3 * (STEPS - 3) + 1))
            dve.wait_ge(s["h_hi_ready"], STEPS)
            nc.vector.tensor_tensor(h16[:, 1, 1, :], h32[:, 1, :], h16[:, 1, 0, :], ALU.subtract
                                    ).then_inc(s["h_lo_ready"], 1)
            summed = 3 * (STEPS - 2)
            for j, sums in enumerate((("dve_drained", done + 1), ("dve_drained", done + 2),
                                      ("y_added", summed + 1), ("y_added", summed + 2))):
                close(4 + j, j, OT - 1, sums)
            for j in range(HT):
                final_scale(NH - 1, j)
            for j in (2, 3):
                dve.wait_ge(s["final_scaled"], (NH - 1) * HT + j + 1)
                dve.wait_ge(s["residual_landed"], 16 * NH)
                dve.wait_ge(s["final_ready"], (NH - 1) * HT + j)
                nc.vector.tensor_tensor(x_res[:, j, :], ysum[:, j, rows], x_res[:, j, :], ALU.add
                                        ).then_inc(s["final_ready"], 1)

        @block.tensor
        def _(pe):
            PAIRS = ((0, 0), (0, 1), (1, 0))

            def transpose_xn(c, t):
                if not (isinstance(c, int) and c * TPC + t < 2):
                    pe.wait_ge(s["xn_stored"], c * TPC + t - 1)
                pe.wait_ge(s["xn_lo_ready"], c * TPC + t + 1)
                for part in range(2):
                    for i in range(HT):
                        last = nc.tensor.transpose(
                            xn_ps[:, t % 2, part, i, :],
                            xn16[:, (c * TPC + t) % (2 * TPC), part, i * P:(i + 1) * P], ident[:])
                last.then_inc(s["xn_transposed"], 1)

            def project_qk(c):
                pe.wait_ge(s["xn_stored"], (c + 1) * TPC)
                for n, name in ((0, "q_product"), (1, "k_product")):
                    if not first(c):
                        pe.wait_ge(s["qkv32_ready"], c * 3 - 2 + n)
                    for i in range(HT):
                        for w, a in PAIRS:
                            last = nc.tensor.matmul(qkv_ps[:, n, :],
                                                    wqkv16[:, w, i, n * D:(n + 1) * D],
                                                    xnT[:, a, i, bass.ds(c * CHUNK, CHUNK)],
                                                    start=(i == 0 and (w, a) == (0, 0)),
                                                    stop=(i == HT - 1 and (w, a) == (1, 0)))
                    last.then_inc(s[name], 1)

            def project_v(c, tiles):
                if not first(c) and tiles[0] == 0:
                    pe.wait_ge(s["qkv32_ready"], c * 3)
                for t in tiles:
                    for i in range(HT):
                        for a, w in PAIRS:
                            last = nc.tensor.matmul(qkv_ps[:, 2, t * D:(t + 1) * D],
                                                    xnT[:, a, i, bass.ds(c * CHUNK + t * P, P)],
                                                    wqkv16[:, w, i, 2 * D:3 * D],
                                                    start=(i == 0 and (a, w) == (0, 0)),
                                                    stop=(i == HT - 1 and (a, w) == (1, 0)))
                if tiles[-1] == TPC - 1:
                    last.then_inc(s["v_product"], 1)

            def max_scores(n, item):
                if not (isinstance(n, int) and n == 0 and item < 2):
                    pe.wait_ge(s["max_reduced"], n * RT + item - 1)
                q0, key0 = n * CHUNK + (item % 4) * P, (item // 4) * CHUNK
                nc.tensor.matmul(max_ps[:, item % 2, :], q16[:, 0, bass.ds(q0, P)],
                                 k16[:, 0, key0:key0 + CHUNK],
                                 start=True, stop=True).then_inc(s["max_product"], 1)

            pe.wait_ge(s["identity_ready"], 1)
            for t in range(TPC):
                transpose_xn(0, t)
            pe.wait_ge(s["w16_ready"], 1)
            for c in range(NC):
                if c == 0:
                    pe.wait_ge(s["scales_ready"], 1)
                project_qk(c)
                if c == 0:
                    project_v(0, range(TPC))
                    for t in range(TPC):
                        transpose_xn(1, t)
                    continue
                for pair in ((0, 1), (2, 3)):
                    for t in pair:
                        if c + 1 < NC:
                            transpose_xn(c + 1, t)
                    for t in pair:
                        max_scores(0, (c - 1) * TPC + t)
                    project_v(c, pair)
            pe.wait_ge(s["qkv_hi_ready"], NC * 3 - 1)
            for t in range(TPC):
                max_scores(0, (NC - 1) * TPC + t)

            pe.wait_ge(s["consts_ready"], 1)
            pe.wait_ge(s["qkv_lo_ready"], 3 * NC - 1)
            pe.wait_ge(s["w16_ready"], 2)

            def scores(n, k):
                if not first(n) or k >= 4:
                    pe.wait_ge(s["exp16_done"], n * RT + k - 3)
                for i, (a, b) in enumerate(PAIRS):
                    nc.tensor.matmul(score_ps[:, k % 4, :], k16[:, a, k * P:(k + 1) * P],
                                     q16[:, b, bass.ds(n * CHUNK, CHUNK)], start=(i == 0), stop=False)
                if k == 0:
                    pe.wait_ge(s["shift_ready"], n + 1)
                nc.tensor.matmul(score_ps[:, k % 4, :], shift_up[:],
                                 neg_max[:, bass.ds(n, 1), :].rearrange("p a q -> p (a q)"),
                                 start=False, stop=True).then_inc(s["score_product"], 1)

            def weighted_values(n, k):
                if k == 0 and first(n):
                    pe.wait_ge(s["qkv_lo_ready"], 3 * NC)
                pe.wait_ge(s["p_lo_ready"], n * RT + k + 1)
                if k == 0 and not first(n):
                    pe.wait_ge(s["o_copied"], n)
                for i, (a, b) in enumerate(PAIRS):
                    last = nc.tensor.matmul(o_ps[:], v16[:, a, k, :], p16[:, k % 4, b, :],
                                            start=(k == 0 and i == 0), stop=(k == RT - 1 and i == 2))
                last.then_inc(s["pv_product"], 1)

            def spread_sum(m):
                pe.wait_ge(s["sum_split"], m + 1)
                if not first(m):
                    pe.wait_ge(s["attn_stored"], m * HT)
                for part in range(2):
                    last = nc.tensor.matmul(tail_ps[:], ones16[:], p_sum16[:, part, :],
                                            start=(part == 0), stop=(part == 1))
                last.then_inc(s["sum_spread"], 1)

            def attention_out(m, j):
                if j == 0:
                    pe.wait_ge(s["o_lo_ready"], m + 1)
                else:
                    pe.wait_ge(s["attn_stored"], m * HT + j)
                for i, (a, b) in enumerate(PAIRS):
                    last = nc.tensor.matmul(tail_ps[:], wo16[:, a, j * P:(j + 1) * P], o16[:, b, :],
                                            start=(i == 0), stop=(i == 2))
                last.then_inc(s["attn_product"], 1)

            def attention(n, with_previous, with_next):
                item = 0
                for k in range(RT):
                    if k >= LAG:
                        weighted_values(n, k - LAG)
                    elif with_previous:
                        weighted_values(n - 1, RT + k - LAG)
                    scores(n, k)
                    if with_next:
                        for _ in range(MAX_ITEMS[k]):
                            max_scores(n + 1, item)
                            item += 1
                    if with_previous:
                        if k == INVERT_AT - 1:
                            spread_sum(n - 1)
                        if k >= OUT_AT:
                            attention_out(n - 1, k - OUT_AT)

            attention(0, False, True)
            with pe.Fori(1, NC - 1) as n:
                attention(n, True, True)
            attention(NC - 1, True, False)
            for k in range(RT - LAG, RT):
                weighted_values(NC - 1, k)

            def drained(t, order, at):
                item = order[at]
                if item in ACT_DRAINS:
                    own = [x for x in ACT_DRAINS if x in order].index(item)
                    pe.wait_ge(s["act_drained"], act_drains_before(t) + own + 1)
                else:
                    own = [x for x in order if x in DVE_DRAINS].index(item)
                    pe.wait_ge(s["dve_drained"], dve_drains_before(t) + own + 1)

            def gate_up_product(t, order, at, tile, rows):
                kind, g = order[at]
                w16 = gate16 if kind == "g" else up16
                for half in range(2):
                    r0 = rows + half * CHUNK
                    for part in range(2):
                        last = nc.tensor.matmul(ffn_ps[:, slot_of(t, at), half, :],
                                                w16[:, g, bass.ds(tile * P, P)],
                                                xnT[:, part, g, r0:r0 + CHUNK],
                                                start=(part == 0), stop=(part == 1))
                last.then_inc(s["ffn_product"], 1)

            def down_product(slot, j, tile, h_parity):
                for half in range(2):
                    for part in range(2):
                        last = nc.tensor.matmul(
                            ffn_ps[:, slot, half, :],
                            down16[:, bass.ds(tile, 1), j * P:(j + 1) * P].rearrange("p a b -> p (a b)"),
                            h16[:, h_parity, part, half * CHUNK:(half + 1) * CHUNK],
                            start=(part == 0), stop=(part == 1))
                last.then_inc(s["ffn_product"], 1)

            def opening_step(t, at):
                n = t * len(OPEN) + at - (RING - 1)
                if n >= 0:
                    drained(n // len(OPEN), OPEN, n % len(OPEN))
                gate_up_product(t, OPEN, at, t, 0)

            def ffn_step(t, parity, tile, y_tile, rows):
                for at in range(len(FULL)):
                    if at >= RING:
                        drained(t, FULL, at - RING)
                    elif isinstance(t, int) and t == 2:
                        if at < RING - 1:
                            drained(1, OPEN, len(OPEN) - (RING - 1) + at)
                        else:
                            pe.wait_ge(s["attn_stored"], NC * HT)
                    else:
                        drained(t - 1, FULL, len(FULL) + at - RING)
                    kind, j = FULL[at]
                    if kind != "y":
                        gate_up_product(t, FULL, at, tile, rows)
                        continue
                    if j == 0:
                        pe.wait_ge(s["h_lo_ready"], t - 1)
                    down_product(at % RING, j, y_tile, parity)

            pe.wait_ge(s["int4_landed"], 3 * 16)
            pe.wait_ge(s["exp16_done"], NC * RT)
            for at in range(3):
                if at == 0:
                    pe.wait_ge(s["o_copied"], NC)
                opening_step(0, at)
            spread_sum(NC - 1)
            for at in range(3, len(OPEN)):
                opening_step(0, at)
            opening_step(1, 0)
            opening_step(1, 1)
            for j in range(HT):
                attention_out(NC - 1, j)
                opening_step(1, 2 + j)
            opening_step(1, 6)
            opening_step(1, 7)
            ffn_step(2, 0, 2, 0, 0)
            ffn_step(3, 1, 3, 1, 0)
            with pe.Fori(2, OT // 2) as pair:
                ffn_step(pair * 2, 0, pair * 2, pair * 2 - 2, 0)
                ffn_step(pair * 2 + 1, 1, pair * 2 + 1, pair * 2 - 1, 0)
            ffn_step(OT, 0, 0, OT - 2, HALF)
            ffn_step(OT + 1, 1, 1, OT - 1, HALF)
            with pe.Fori(OT // 2 + 1, OT) as pair:
                ffn_step(pair * 2, 0, pair * 2 - OT, pair * 2 - OT - 2, HALF)
                ffn_step(pair * 2 + 1, 1, pair * 2 + 1 - OT, pair * 2 - OT - 1, HALF)
            for j in (2, 3, 0, 1):
                if j == 2:
                    pe.wait_ge(s["h_lo_ready"], STEPS - 1)
                drained(STEPS - 1, FULL, len(FULL) + j - RING)
                down_product(j, j, OT - 2, 0)
            pe.wait_ge(s["h_lo_ready"], STEPS)
            for j in range(HT):
                if j < 2:
                    pe.wait_ge(s["dve_drained"], dve_drains_before(STEPS) + j + 1)
                else:
                    pe.wait_ge(s["act_drained"], act_drains_before(STEPS) + j - 1)
                down_product(j, j, OT - 1, 1)


def kernel(L0_attn_x, L0_attn_Wqkv, L0_attn_bqkv, L0_attn_Wo, L0_attn_bo, L0_ffn_gate_q,
           L0_ffn_gate_s, L0_ffn_up_q, L0_ffn_up_s, L0_ffn_down_q, L0_ffn_down_s):
    import numpy as np
    import concourse.bacc as bacc
    from concourse.bass_utils import run_bass_kernel_spmd

    def columns(a, width):
        a = np.asarray(a).reshape(-1, P, width)
        return a.transpose(1, 0, 2)

    def grouped(q):
        q = np.asarray(q)
        return q.T.reshape(-1, P, q.shape[0]).transpose(1, 0, 2)

    x = np.asarray(L0_attn_x)[0]
    arrays = {
        "x": x, "xT": x.T, "wqkv": L0_attn_Wqkv,
        "bqkv": columns(L0_attn_bqkv, 1)[:, :, 0], "wo": L0_attn_Wo,
        "bo": columns(L0_attn_bo, 1)[:, :, 0],
        "gate_q": grouped(L0_ffn_gate_q), "gate_s": columns(L0_ffn_gate_s, HT),
        "up_q": grouped(L0_ffn_up_q), "up_s": columns(L0_ffn_up_s, HT),
        "down_q": grouped(L0_ffn_down_q), "down_s": columns(L0_ffn_down_s, OT),
    }
    arrays = {name: np.ascontiguousarray(a) for name, a in arrays.items()}
    nc = bacc.Bacc("TRN2", target_bir_lowering=False, num_devices=1)
    args = [nc.dram_tensor(name, a.shape, mybir.dt.from_np(a.dtype), kind="ExternalInput").ap()
            for name, a in arrays.items()]
    out = nc.dram_tensor("outT", (HID, ROWS), F32, kind="ExternalOutput").ap()
    build(nc, *args, out)
    result = run_bass_kernel_spmd(nc, [arrays], core_ids=[0])
    return np.asarray(result.results[0]["outT"]).T[None]
```

```python
from contextlib import ExitStack

import concourse.bass as bass
from concourse import mybir

F32 = mybir.dt.float32
F16 = mybir.dt.float16
BF16 = mybir.dt.bfloat16
I32 = mybir.dt.int32
ALU = mybir.AluOpType
ACT = mybir.ActivationFunctionType
AX_X = mybir.AxisListType.X
AX_XY = mybir.AxisListType.XY
ABSMAX = bass.bass_isa.ReduceOp.absmax

P = 128
ROWS = 2048
HID = 512
D = HID // 4
INNER = 1792
LN_EPS = 1e-5

HT = HID // P
OT = INNER // P
RT = ROWS // P
CHUNK = 512
NC = ROWS // CHUNK
TPC = CHUNK // P
HALF = 1024
NH = ROWS // HALF

X_EXP = 11
X_SCALE = float(2 ** X_EXP)
PROB_EXP = 8
SHIFT_EXP = 22
LN2 = 0.6931471805599453
QKV_L1 = 512.0
FFN_L1 = 4096.0
SCALE_BITS = float((127 + 14 + 127) << 23)
INVERSE_BITS = float((127 + 127) << 23)

FULL = [("g", 0), ("u", 0), ("y", 0), ("g", 1), ("u", 1), ("y", 1),
        ("g", 2), ("u", 2), ("y", 2), ("g", 3), ("u", 3), ("y", 3)]
ACT_DRAINS = [("g", 0), ("u", 0), ("y", 1), ("y", 2), ("y", 3)]
OPEN = [[("g", 0), ("u", 0), ("g", 1), ("g", 3), ("u", 1), ("u", 3), ("g", 2), ("u", 2)],
        [x for x in FULL if x[0] != "y"]]
OPEN_ACT_DRAINS = [[("g", 0), ("u", 0), ("g", 3), ("u", 3)], [("g", 0), ("u", 0)]]
RING = 4
STEPS = NH * OT

MAX_ITEMS = [2, 1, 1, 2, 1, 0, 1, 1, 1, 1, 1, 1, 1, 2, 0, 0]
FIRST_ITEMS = [1, 1, 1, 1, 1, 1, 1, 1, 1, 2, 1, 1, 1, 2, 0, 0]
SHIFT_AT = 13
INVERT_AT = 4
OUT_AT = 12
LAG = 3


def before(step, of, opening):
    if isinstance(step, int) and step <= 2:
        return sum(opening[:step])
    return (step - 2) * of + sum(opening)


def items_of(chunk):
    return FIRST_ITEMS if isinstance(chunk, int) and chunk == 0 else MAX_ITEMS


def order_of(step):
    return OPEN[step] if isinstance(step, int) and step < 2 else FULL


def act_drains_of(step):
    return OPEN_ACT_DRAINS[step] if isinstance(step, int) and step < 2 else ACT_DRAINS


def slot_of(step, at):
    if isinstance(step, int) and step < 2:
        return (step * len(OPEN[0]) + at + 2) % (RING - 1)
    return at % RING


def products_before(step):
    return before(step, len(FULL), [len(x) for x in OPEN])


def act_drains_before(step):
    return before(step, len(ACT_DRAINS), [len(x) for x in OPEN_ACT_DRAINS])


def dve_drains_before(step):
    return before(step, len(FULL) - len(ACT_DRAINS),
                  [len(x) - len(a) for x, a in zip(OPEN, OPEN_ACT_DRAINS)])


def build(nc, x, xT, wqkv, bqkv, wo, bo, gate_q, gate_s, up_q, up_s, down_q, down_s, outT):
    ctx = ExitStack()
    with ctx:
        def sb(name, shape, dt, scope=ctx):
            return scope.enter_context(nc.sbuf_tensor(name, shape, dt))

        def pb(name, shape, dt, scope=ctx):
            return scope.enter_context(nc.psum_tensor(name, shape, dt))

        def sem(name):
            return ctx.enter_context(nc.semaphore(name))

        gate16 = sb("gate16", [P, HT, INNER], F16)
        up16 = sb("up16", [P, HT, INNER], F16)
        down16 = sb("down16", [P, OT, HID], F16)
        xnT = sb("xnT", [P, 2, HT, ROWS], F16)
        attnT = sb("attnT", [P, HT, ROWS], F32)
        gate_col = sb("gate_col", [P, OT, HT], F32)
        up_col = sb("up_col", [P, OT, HT], F32)
        down_col = sb("down_col", [P, HT, OT], F32)
        gate_dq = sb("gate_dq", [P, OT, HT], F32)
        up_dq = sb("up_dq", [P, OT, HT], F32)
        down_dq = sb("down_dq", [P, HT, OT], F32)
        bo_col = sb("bo_col", [P, HT], F32)
        bqkv_col = sb("bqkv_col", [P, 3], F32)
        bqkv_sc = sb("bqkv_sc", [P, 3], F32)
        ident = sb("ident", [P, P], F16)
        ones16 = sb("ones16", [P, P], F16)
        shift_up = sb("shift_up", [P, P], BF16)
        shift_less = sb("shift_less", [P, 1], F32)
        max_less = sb("max_less", [P, TPC], F32)
        absmax = sb("absmax", [P, 5], F32)
        absmax_all = sb("absmax_all", [P, 5], F32)
        bound = sb("bound", [P, 4], F32)
        fit = sb("fit", [P, 4], F32)
        unfit = sb("unfit", [P, 4], F32)
        qkv_unscale = sb("qkv_unscale", [P, 1], F32)
        exp_one = sb("exp_one", [P, 1], F32)
        exp_scale = sb("exp_scale", [P, 1], F32)
        attn_unscale = sb("attn_unscale", [P, 1], F32)

        rows_scope = ExitStack()
        x_rows = sb("x_rows", [P, RT, HID], F32, rows_scope)
        rows_scope.close()
        ysum = sb("ysum", [P, HT, ROWS], F32)

        att = ExitStack()
        q16 = sb("q16", [P, 2, ROWS], F16, att)
        k16 = sb("k16", [P, 2, ROWS], F16, att)
        v16 = sb("v16", [P, 2, RT, D], F16, att)
        late = ExitStack()
        p32 = sb("p32", [P, 4, CHUNK], F32, late)
        p16 = sb("p16", [P, 4, 2, CHUNK], F16, late)
        wo16 = sb("wo16", [P, 2, HID], F16, late)
        max_parts = sb("max_parts", [P, TPC, 4], F32, late)
        max_col = sb("max_col", [P, TPC], F32, late)
        tail = ExitStack()
        p_sum = sb("p_sum", [P, CHUNK], F32, tail)
        p_sum16 = sb("p_sum16", [P, 2, CHUNK], F16, tail)
        neg_max = sb("neg_max", [P, NC, CHUNK], F16, tail)
        o_raw = sb("o_raw", [P, CHUNK], F32, tail)
        o_norm = sb("o_norm", [P, CHUNK], F32, tail)
        o32 = sb("o32", [P, CHUNK], F32, tail)
        o16 = sb("o16", [P, 2, CHUNK], F16, tail)
        inv_sum = sb("inv_sum", [P, CHUNK], F32, tail)
        tail.close()
        late.close()
        early = ExitStack()
        xn16 = sb("xn16", [P, 2 * TPC, 2, HID], F16, early)
        kept = ExitStack()
        sb("over_wo16_max", [P, 1024 + 64], F16, kept)
        wqkv16 = sb("wqkv16", [P, 2, HT, 3 * D], F16, kept)
        wqkv32 = sb("wqkv32", [P, HT, 3 * D], F32, kept)
        wo32 = sb("wo32", [P, HID], F32, kept)
        qkv32 = sb("qkv32", [P, 3, CHUNK], F32, kept)
        bn6 = sb("bn6", [P, RT, 6], F32, kept)
        mean_var = sb("mean_var", [P, RT, 2], F32, kept)
        var_eps = sb("var_eps", [P, RT], F32, kept)
        std = sb("std", [P, RT], F32, kept)
        rstd0 = sb("rstd0", [P, RT], F32, kept)
        newton = sb("newton", [P, RT], F32, kept)
        newton2 = sb("newton2", [P, RT], F32, kept)
        newton3 = sb("newton3", [P, RT], F32, kept)
        x_mul = sb("x_mul", [P, RT], F32, kept)
        x_add = sb("x_add", [P, RT], F32, kept)
        kept.close()
        early.close()
        att.close()

        ffn = ExitStack()
        g32 = sb("g32", [P, 2, HALF], F32, ffn)
        u32 = sb("u32", [P, 2, HALF], F32, ffn)
        silu32 = sb("silu32", [P, HALF], F32, ffn)
        h32 = sb("h32", [P, 2, HALF], F32, ffn)
        h16 = sb("h16", [P, 2, 2, HALF], F16, ffn)
        x_res = sb("x_res", [P, HT, HALF], F32, ffn)
        y_part = sb("y_part", [P, 3, HALF], F32, ffn)
        ffn.close()

        front = ExitStack()
        xn_ps = pb("xn_ps", [P, 2, 2, HT, P], F16, front)
        qkv_ps = pb("qkv_ps", [P, 3, CHUNK], F32, front)
        front.close()
        attps = ExitStack()
        score_ps = pb("score_ps", [P, 4, CHUNK], F32, attps)
        o_ps = pb("o_ps", [P, CHUNK], F32, attps)
        max_ps = pb("max_ps", [P, 2, CHUNK], F32, attps)
        tail_ps = pb("tail_ps", [P, CHUNK], F32, attps)
        attps.close()
        ffn_ps = pb("ffn_ps", [P, RING, 2, CHUNK], F32)

        names = """weights_landed wo_landed scales_landed residual_landed int4_landed out_stored
            identity_zeroed identity_ready consts_ready absmax_ready absmax_spread
            qkv_scales_ready scales_ready fit_ready first_hi_ready first_ready xn32_done w16_hi
            w16_ready wo16_hi stats_ready var_ready std_ready moments_ready xn32_ready
            xn_hi_ready xn_lo_ready xn_transposed xn_stored q_product k_product v_product
            qkv32_ready qkv_hi_ready qkv_lo_ready max_product max_reduced max_done max_moved
            shift_ready score_product exp32_done exp16_done p_lo_ready pv_product p_summed
            sum_hi_ready sum_split sum_spread sum_inverted o_copied o_scaled o_hi_ready
            o_lo_ready attn_product attn_stored dve_small ysum_zeroed ffn_product act_drained
            dve_drained silu_done h_ready h_hi_ready h_lo_ready y_added final_silu final_scaled
            final_ready last_ready last_h_lo_ready last_stored opening_added""".split()
        s = {n: sem(n) for n in names}
        x_landed = [sem(f"x_landed_{c}") for c in range(NC)]

        last_group = ysum[:, 0:2, (NH - 1) * HALF:]

        def first(n):
            return isinstance(n, int) and n == 0

        POOL_LAST = [(0, 0), (0, 1), (1, 0), (1, 1), (2, 0)]
        DVE_LAST = [(2, 1), (3, 0), (3, 1)]
        outv = outT.rearrange("(j p) r -> p j r", p=P)

        def store_last(engine, j, part):
            r0 = part * CHUNK
            return engine.dma_start(outv[:, j, HALF + r0:HALF + r0 + CHUNK], x_res[:, j, r0:r0 + CHUNK])

        def add_residual(engine, j, part):
            xr = x_res[:, j, part * CHUNK:(part + 1) * CHUNK]
            r0 = (NH - 1) * HALF + part * CHUNK
            return engine.tensor_tensor(xr, ysum[:, j, r0:r0 + CHUNK], xr, ALU.add)

        block = ctx.enter_context(nc.Block())

        @block.sync
        def _(sp):
            xv = x.rearrange("(t p) h -> p t h", p=P)
            for c in range(NC):
                if c == 1:
                    sp.wait_ge(s["weights_landed"], 16)
                    sp.wait_ge(s["wo_landed"], 16)
                if c:
                    sp.wait_ge(x_landed[c - 1], 16)
                sp.dma_start(x_rows[:, c * TPC:(c + 1) * TPC, :],
                             xv[:, c * TPC:(c + 1) * TPC, :]).then_inc(x_landed[c], 16)
            xTv = xT.rearrange("(j p) r -> p j r", p=P)
            sp.wait_ge(s["attn_stored"], NC * HT)
            sp.dma_start(x_res[:], xTv[:, :, :HALF]).then_inc(s["residual_landed"], 16)
            for j in range(HT):
                sp.wait_ge(s["final_ready"], j + 1)
                sp.dma_start(outv[:, j, :HALF], x_res[:, j, :]).then_inc(s["out_stored"], 16)
            sp.wait_ge(s["out_stored"], 16 * HT)
            sp.dma_start(x_res[:], xTv[:, :, HALF:]).then_inc(s["residual_landed"], 16)
            for i, (j, part) in enumerate(POOL_LAST):
                sp.wait_ge(s["final_ready"], HT + i + 1)
                store_last(sp, j, part).then_inc(s["out_stored"], 16)
            sp.wait_ge(s["out_stored"], 16 * (HT + len(POOL_LAST)))

        @block.gpsimd
        def _(pool):
            nc.gpsimd.memset(ident[:], 0.0).then_inc(s["identity_zeroed"], 1)
            nc.gpsimd.memset(ones16[:], 1.0)
            nc.gpsimd.memset(shift_up[:], float(2 ** SHIFT_EXP)).then_inc(s["consts_ready"], 1)
            pool.wait_ge(s["identity_zeroed"], 1)
            nc.gpsimd.affine_select(out=ident[:], in_=ident[:], compare_op=ALU.not_equal, fill=1.0,
                                    base=0, pattern=[[-1, P]], channel_multiplier=1
                                    ).then_inc(s["identity_ready"], 1)
            pool.wait_ge(s["absmax_ready"], 1)
            nc.gpsimd.partition_all_reduce(absmax_all[:], absmax[:], P, ABSMAX
                                           ).then_inc(s["absmax_spread"], 1)

            for t in range(1, RT):
                if t == 2 * TPC:
                    for dst, src in ((gate16, gate_q), (up16, up_q), (down16, down_q)):
                        pool.dma_start(dst[:], src).then_inc(s["int4_landed"], 16)
                if t % TPC == 0 or t == 1:
                    pool.wait_ge(s["moments_ready"], t // TPC + 1)
                if t >= 2 * TPC:
                    pool.wait_ge(s["xn_transposed"], t - 2 * TPC + 1)
                nc.gpsimd.tensor_scalar(xn16[:, t % (2 * TPC), 0, :], x_rows[:, t, :],
                                        x_mul[:, t:t + 1], x_add[:, t:t + 1],
                                        ALU.mult, ALU.add).then_inc(s["xn_hi_ready"], 1)
                if t < 2 * TPC:
                    continue
                pool.wait_ge(s["xn_hi_ready"], t)
                nc.gpsimd.tensor_scalar(x_rows[:, t, :], x_rows[:, t, :],
                                        x_mul[:, t:t + 1], x_add[:, t:t + 1],
                                        ALU.mult, ALU.add).then_inc(s["xn32_ready"], 1)
            pool.wait_ge(s["xn_lo_ready"], RT)
            nc.gpsimd.memset(ysum[:], 0.0).then_inc(s["ysum_zeroed"], 1)

            def sum_probabilities(n):
                for k in range(1, RT):
                    pool.wait_ge(s["exp32_done"], n * RT + k + 1)
                    if k == 1:
                        if not first(n):
                            pool.wait_ge(s["sum_split"], n)
                        total = p32[:, 0, :]
                    else:
                        pool.wait_ge(s["p_summed"], n * (RT - 1) + k - 1)
                        total = p_sum[:]
                    nc.gpsimd.tensor_tensor(p_sum[:], total, p32[:, k % 4, :], ALU.add
                                            ).then_inc(s["p_summed"], 1)

            sum_probabilities(0)
            with pool.Fori(1, NC) as n:
                sum_probabilities(n)

            def add(t, j, rows, drained):
                pool.wait_ge(s["act_drained"], drained)
                if not (isinstance(t, int) and t == 2):
                    pool.wait_ge(s["y_added"], (t - 3) * 3 + j)
                nc.gpsimd.tensor_tensor(ysum[:, j, rows], ysum[:, j, rows], y_part[:, j - 1, :],
                                        ALU.add).then_inc(s["y_added"], 1)

            def ffn_step(t, parity, half, last=False):
                with_y = half is not None
                if with_y:
                    rows = slice(half * HALF, (half + 1) * HALF)
                    if not last:
                        add(t, 1, rows, act_drains_before(t) + 3)
                pool.wait_ge(s["h_hi_ready"], t)
                nc.gpsimd.tensor_tensor(h16[:, parity, 1, :], h32[:, parity, :],
                                        h16[:, parity, 0, :], ALU.subtract).then_inc(s["h_lo_ready"], 1)
                if with_y:
                    if last:
                        add(t, 1, rows, act_drains_before(t) + 3)
                    add(t, 2, rows, act_drains_before(t) + 4)
                    add(t, 3, rows, act_drains_before(t) + 5)

            def final_add(j):
                rows = slice(0, HALF)
                pool.wait_ge(s["final_scaled"], j * 2 + 2)
                pool.wait_ge(s["residual_landed"], 16)
                xr = x_res[:, bass.ds(j, 1), :].rearrange("p a r -> p (a r)")
                ys = ysum[:, bass.ds(j, 1), rows].rearrange("p a r -> p (a r)")
                nc.gpsimd.tensor_tensor(xr, ys, xr, ALU.add).then_inc(s["final_ready"], 1)

            for i, dst in enumerate((g32, u32)):
                pool.wait_ge(s["act_drained"], 3 + i)
                pool.wait_ge(s["dve_drained"], 3 + i)
                nc.gpsimd.tensor_tensor(dst[:, 0, :], dst[:, 0, :], last_group[:, i, :], ALU.add
                                        ).then_inc(s["opening_added"], 1)
            ffn_step(1, 0, None)
            pool.wait_ge(s["opening_added"], 2)
            nc.gpsimd.memset(last_group, 0.0).then_inc(s["ysum_zeroed"], 1)
            pool.wait_ge(s["ysum_zeroed"], 2)
            ffn_step(2, 1, 0)
            ffn_step(3, 0, 0)
            with pool.Fori(2, OT // 2) as pair:
                ffn_step(pair * 2, 1, 0)
                ffn_step(pair * 2 + 1, 0, 0)
            ffn_step(OT, 1, 0)
            ffn_step(OT + 1, 0, 0)
            ffn_step(OT + 2, 1, 1)
            ffn_step(OT + 3, 0, 1)
            with pool.Fori(0, HT) as j:
                ffn_step(j * 2 + OT + 4, 1, 1)
                ffn_step(j * 2 + OT + 5, 0, 1)
                final_add(j)
            ffn_step(STEPS - 2, 1, 1)
            ffn_step(STEPS - 1, 0, 1, last=True)
            rows = slice((NH - 1) * HALF, NH * HALF)
            add(STEPS, 2, rows, act_drains_before(STEPS) + 1)
            add(STEPS, 3, rows, act_drains_before(STEPS) + 2)
            pool.wait_ge(s["residual_landed"], 16 * NH)
            for j, part in POOL_LAST:
                pool.wait_ge(s["final_scaled"], ((NH - 1) * HT + j) * 2 + part + 1)
                add_residual(nc.gpsimd, j, part).then_inc(s["final_ready"], 1)

        @block.scalar
        def _(act):
            act.dma_start(wqkv32[:], wqkv.rearrange("(i p) f -> p i f", p=P)
                          ).then_inc(s["weights_landed"], 16)
            act.dma_start(bqkv_col[:], bqkv).then_inc(s["scales_landed"], 16)
            act.dma_start(gate_col[:], gate_s).then_inc(s["scales_landed"], 16)
            act.dma_start(up_col[:], up_s).then_inc(s["scales_landed"], 16)
            act.dma_start(wo32[:], wo).then_inc(s["wo_landed"], 16)
            act.dma_start(bo_col[:], bo).then_inc(s["scales_landed"], 16)
            act.dma_start(down_col[:], down_s).then_inc(s["scales_landed"], 16)

            def square_root(c):
                tiles = slice(c * TPC, (c + 1) * TPC)
                act.wait_ge(s["var_ready"], c + 1)
                nc.scalar.activation(std[:, tiles], var_eps[:, tiles], ACT.Sqrt
                                     ).then_inc(s["std_ready"], 1)

            def store_transposed(c, tiles):
                for t in tiles:
                    act.wait_ge(s["xn_transposed"], c * TPC + t + 1)
                    nc.scalar.activation(xnT[:, :, :, bass.ds(c * CHUNK + t * P, P)],
                                         xn_ps[:, t % 2, :, :, :], ACT.Copy
                                         ).then_inc(s["xn_stored"], 1)

            def store_qk(c):
                for i, (product, dst) in enumerate((("k_product", k16), ("q_product", q16))):
                    act.wait_ge(s[product], c + 1)
                    if not first(c):
                        act.wait_ge(s["qkv_lo_ready"], c * 3 - 2 + i)
                    args = dict(scale=qkv_unscale[:, 0:1], bias=bqkv_sc[:, 1 - i:2 - i])
                    nc.scalar.activation(dst[:, 0, bass.ds(c * CHUNK, CHUNK)], qkv_ps[:, i, :],
                                         ACT.Identity, **args).then_inc(s["qkv_hi_ready"], 1)
                    nc.scalar.activation(qkv32[:, i, :], qkv_ps[:, i, :], ACT.Identity, **args
                                         ).then_inc(s["qkv32_ready"], 1)

            def store_v(c):
                act.wait_ge(s["v_product"], c + 1)
                if not first(c):
                    act.wait_ge(s["qkv_lo_ready"], c * 3)
                nc.scalar.activation(v16[:, 0, bass.ds(c * TPC, TPC), :],
                                     qkv_ps[:, 2, :].rearrange("p (t d) -> p t d", d=D), ACT.Copy,
                                     scale=qkv_unscale[:, 0:1]).then_inc(s["qkv_hi_ready"], 1)
                nc.scalar.activation(qkv32[:, 2, :], qkv_ps[:, 2, :], ACT.Copy,
                                     scale=qkv_unscale[:, 0:1]).then_inc(s["qkv32_ready"], 1)

            square_root(0)
            act.wait_ge(s["moments_ready"], 1)
            nc.scalar.activation(xn16[:, 0, 0, :], x_rows[:, 0, :], ACT.Identity,
                                 scale=x_mul[:, 0:1], bias=x_add[:, 0:1]
                                 ).then_inc(s["first_hi_ready"], 1)
            act.wait_ge(s["first_hi_ready"], 1)
            nc.scalar.activation(x_rows[:, 0, :], x_rows[:, 0, :], ACT.Identity,
                                 scale=x_mul[:, 0:1], bias=x_add[:, 0:1]
                                 ).then_inc(s["first_ready"], 1)
            act.wait_ge(s["fit_ready"], 1)
            nc.scalar.activation(wqkv16[:, 0, :, :], wqkv32[:], ACT.Copy, scale=fit[:, 0:1]
                                 ).then_inc(s["w16_hi"], 1)
            store_transposed(0, range(TPC))
            nc.scalar.activation(wo16[:, 0, :], wo32[:], ACT.Copy, scale=fit[:, 1:2]
                                 ).then_inc(s["wo16_hi"], 1)
            square_root(1)
            act.wait_ge(s["qkv_scales_ready"], 1)
            for c in range(NC):
                store_qk(c)
                if c == 1:
                    store_transposed(2, (0, 1))
                    square_root(3)
                    store_transposed(2, (2, 3))
                elif c + 1 < NC:
                    store_transposed(c + 1, range(TPC))
                if c == 0:
                    square_root(2)
                store_v(c)

            def exponentials(n, k):
                act.wait_ge(s["score_product"], n * RT + k + 1)
                if not first(n) or k >= 4:
                    act.wait_ge(s["p_lo_ready"], n * RT + k - 3)
                    if k >= 4:
                        act.wait_ge(s["p_summed"], n * (RT - 1) + max(k - 4, 1))
                    else:
                        act.wait_ge(s["p_summed"], n * (RT - 1) + k - 3)
                    act.wait_ge(s["pv_product"], n * RT + k - 3)
                nc.scalar.activation(p32[:, k % 4, :], score_ps[:, k % 4, :], ACT.Exp,
                                     scale=exp_scale[:, 0:1]).then_inc(s["exp32_done"], 1)
                nc.scalar.activation(p16[:, k % 4, 0, :], score_ps[:, k % 4, :], ACT.Exp,
                                     scale=exp_scale[:, 0:1]).then_inc(s["exp16_done"], 1)

            def copy_o(m):
                act.wait_ge(s["pv_product"], (m + 1) * RT)
                nc.scalar.activation(o_raw[:], o_ps[:], ACT.Copy).then_inc(s["o_copied"], 1)

            def add_v_bias(m):
                act.wait_ge(s["o_scaled"], m + 1)
                args = dict(bias=bqkv_sc[:, 2:3])
                nc.scalar.activation(o32[:], o_norm[:], ACT.Identity, **args)
                nc.scalar.activation(o16[:, 0, :], o_norm[:], ACT.Identity, **args
                                     ).then_inc(s["o_hi_ready"], 1)

            def store_attention(m, j):
                act.wait_ge(s["attn_product"], m * HT + j + 1)
                nc.scalar.activation(attnT[:, j, bass.ds(m * CHUNK, CHUNK)], tail_ps[:], ACT.Identity,
                                     scale=attn_unscale[:, 0:1], bias=bo_col[:, j:j + 1]
                                     ).then_inc(s["attn_stored"], 1)

            def attention(n, with_tail):
                for k in range(RT):
                    exponentials(n, k)
                    if with_tail:
                        if k == 1:
                            copy_o(n - 1)
                        if k == INVERT_AT + TPC + 2:
                            add_v_bias(n - 1)
                        if k >= OUT_AT:
                            store_attention(n - 1, k - OUT_AT)

            act.wait_ge(s["scales_ready"], 1)
            nc.scalar.activation(exp_one[:], ident[:, 0:1], ACT.Exp)
            act.wait_ge(s["xn_transposed"], RT)
            attention(0, False)
            with act.Fori(1, NC) as n:
                attention(n, True)

            def drain(t, item, dst, scale):
                at = order_of(t).index(item)
                act.wait_ge(s["ffn_product"], products_before(t) + at + 1)
                src = ffn_ps[:, slot_of(t, at), :, :]
                nc.scalar.activation(dst.rearrange("p (a b) -> p a b", b=CHUNK), src, ACT.Copy,
                                     scale=scale).then_inc(s["act_drained"], 1)

            def start_sums(t, parity, tile):
                if not (isinstance(t, int) and t < 2):
                    act.wait_ge(s["h_ready"], t - 1)
                drain(t, ("g", 0), g32[:, parity, :], gate_dq[:, bass.ds(tile, 1), 0])
                drain(t, ("u", 0), u32[:, parity, :], up_dq[:, bass.ds(tile, 1), 0])

            def silu_of(t, parity):
                if first(t):
                    act.wait_ge(s["opening_added"], 1)
                else:
                    act.wait_ge(s["dve_drained"], dve_drains_before(t + 1) - 1)
                if not first(t):
                    act.wait_ge(s["h_ready"], t)
                nc.scalar.activation(silu32[:], g32[:, parity, :], ACT.Silu).then_inc(s["silu_done"], 1)

            def h_hi(t, parity):
                act.wait_ge(s["h_ready"], t + 1)
                if not (isinstance(t, int) and t < 2):
                    act.wait_ge(s["ffn_product"], products_before(t + 1))
                nc.scalar.activation(h16[:, parity, 0, :], h32[:, parity, :], ACT.Copy
                                     ).then_inc(s["h_hi_ready"], 1)

            def y_drain(t, tile, j):
                if not (isinstance(t, int) and t == 2):
                    act.wait_ge(s["y_added"], (t - 3) * 3 + j)
                drain(t, ("y", j), y_part[:, j - 1, :], down_dq[:, j, bass.ds(tile, 1)])

            def final_silu(half, j):
                rows = slice(half * HALF, (half + 1) * HALF)
                nc.scalar.activation(ysum[:, bass.ds(j, 1), rows], ysum[:, bass.ds(j, 1), rows],
                                     ACT.Silu).then_inc(s["final_silu"], 1)

            def ffn_step(t, parity, tile, y_tile, final=None):
                start_sums(t, parity, tile)
                if final is not None:
                    final_silu(0, final)
                y_drain(t, y_tile, 1)
                h_hi(t - 1, 1 - parity)
                y_drain(t, y_tile, 2)
                silu_of(t, parity)
                y_drain(t, y_tile, 3)

            copy_o(NC - 1)
            act.wait_ge(s["p_summed"], NC * (RT - 1))
            act.wait_ge(s["ysum_zeroed"], 1)

            start_sums(0, 0, 0)
            drain(0, ("g", HT - 1), last_group[:, 0, :], gate_dq[:, 0, HT - 1:HT])
            drain(0, ("u", HT - 1), last_group[:, 1, :], up_dq[:, 0, HT - 1:HT])
            add_v_bias(NC - 1)
            start_sums(1, 1, 1)
            silu_of(0, 0)
            store_attention(NC - 1, 0)
            store_attention(NC - 1, 1)
            h_hi(0, 0)
            store_attention(NC - 1, 2)
            store_attention(NC - 1, 3)
            silu_of(1, 1)
            ffn_step(2, 0, 2, 0)
            ffn_step(3, 1, 3, 1)
            with act.Fori(2, OT // 2) as pair:
                ffn_step(pair * 2, 0, pair * 2, pair * 2 - 2)
                ffn_step(pair * 2 + 1, 1, pair * 2 + 1, pair * 2 - 1)
            ffn_step(OT, 0, 0, OT - 2)
            ffn_step(OT + 1, 1, 1, OT - 1)
            with act.Fori(0, HT) as j:
                ffn_step(j * 2 + OT + 2, 0, j * 2 + 2, j * 2)
                act.wait_ge(s["y_added"], 3 * OT)
                act.wait_ge(s["dve_drained"], dve_drains_before(OT + 1) + 1)
                ffn_step(j * 2 + OT + 3, 1, j * 2 + 3, j * 2 + 1, final=j)
            with act.Fori(OT // 2 + 1 + HT, OT) as pair:
                ffn_step(pair * 2, 0, pair * 2 - OT, pair * 2 - OT - 2)
                ffn_step(pair * 2 + 1, 1, pair * 2 + 1 - OT, pair * 2 - OT - 1)
            h_hi(STEPS - 1, 1)
            for j in (2, 3):
                act.wait_ge(s["y_added"], (STEPS - 3) * 3 + j)
                act.wait_ge(s["ffn_product"], products_before(STEPS) + j + 1)
                nc.scalar.activation(y_part[:, j - 1, :].rearrange("p (a b) -> p a b", b=CHUNK),
                                     ffn_ps[:, j, :, :], ACT.Copy, scale=down_dq[:, j, OT - 2:OT - 1]
                                     ).then_inc(s["act_drained"], 1)
            for j in range(HT):
                act.wait_ge(s["dve_drained"], dve_drains_before(STEPS) + 2 + j + 1)
                final_silu(NH - 1, j)
            for i, (j, part) in enumerate(DVE_LAST):
                act.wait_ge(s["last_ready"], i + 1)
                store_last(act, j, part).then_inc(s["last_stored"], 16)
            act.wait_ge(s["last_stored"], 16 * len(DVE_LAST))

        @block.vector
        def _(dve):
            small = [0]

            def chain(op):
                small[0] += 1
                op.then_inc(s["dve_small"], 1)
                dve.wait_ge(s["dve_small"], small[0])

            def statistics(c):
                dve.wait_ge(x_landed[c], 16)
                for t in range(c * TPC, (c + 1) * TPC):
                    last = nc.vector.bn_stats(bn6[:, t, :], x_rows[:, t, :])
                last.then_inc(s["stats_ready"], 1)

            def variances(c):
                tiles = slice(c * TPC, (c + 1) * TPC)
                dve.wait_ge(s["stats_ready"], c + 1)
                for t in range(tiles.start, tiles.stop):
                    last = nc.vector.bn_aggr(mean_var[:, t, :], bn6[:, t, :])
                chain(last)
                nc.vector.tensor_scalar(var_eps[:, tiles], mean_var[:, tiles, 1], LN_EPS, None, ALU.add
                                        ).then_inc(s["var_ready"], 1)

            def factors(c):
                tiles = slice(c * TPC, (c + 1) * TPC)
                dve.wait_ge(s["std_ready"], c + 1)
                chain(nc.vector.reciprocal(rstd0[:, tiles], std[:, tiles]))
                chain(nc.vector.tensor_tensor(newton[:, tiles], var_eps[:, tiles], rstd0[:, tiles],
                                              ALU.mult))
                chain(nc.vector.tensor_tensor(newton2[:, tiles], newton[:, tiles], rstd0[:, tiles],
                                              ALU.mult))
                chain(nc.vector.tensor_scalar(newton3[:, tiles], newton2[:, tiles], -0.5 * X_SCALE,
                                              1.5 * X_SCALE, ALU.mult, ALU.add))
                chain(nc.vector.tensor_tensor(x_mul[:, tiles], newton3[:, tiles], rstd0[:, tiles],
                                              ALU.mult))
                nc.vector.scalar_tensor_tensor(x_add[:, tiles], mean_var[:, tiles, 0], -1.0,
                                               x_mul[:, tiles], ALU.mult, ALU.mult
                                               ).then_inc(s["moments_ready"], 1)

            def normalise(t):
                dve.wait_ge(s["moments_ready"], t // TPC + 1)
                dve.wait_ge(s["xn_hi_ready"], t)
                nc.vector.tensor_scalar(x_rows[:, t, :], x_rows[:, t, :], x_mul[:, t:t + 1],
                                        x_add[:, t:t + 1], ALU.mult, ALU.add
                                        ).then_inc(s["xn32_done"], 1)

            def split_xn(t):
                if t == 0:
                    dve.wait_ge(s["first_ready"], 1)
                elif t < 2 * TPC:
                    dve.wait_ge(s["xn32_done"], t)
                else:
                    dve.wait_ge(s["xn32_ready"], t - 2 * TPC + 1)
                slot = t % (2 * TPC)
                nc.vector.tensor_tensor(xn16[:, slot, 1, :], x_rows[:, t, :], xn16[:, slot, 0, :],
                                        ALU.subtract).then_inc(s["xn_lo_ready"], 1)

            def split_qk(c, of=(0, 1)):
                for i in of:
                    dst = (k16, q16)[i]
                    dve.wait_ge(s["qkv32_ready"], c * 3 + i + 1)
                    nc.vector.tensor_tensor(dst[:, 1, bass.ds(c * CHUNK, CHUNK)], qkv32[:, i, :],
                                            dst[:, 0, bass.ds(c * CHUNK, CHUNK)],
                                            ALU.subtract).then_inc(s["qkv_lo_ready"], 1)

            def split_v(c):
                dve.wait_ge(s["qkv32_ready"], c * 3 + 3)
                nc.vector.tensor_tensor(v16[:, 1, bass.ds(c * TPC, TPC), :],
                                        qkv32[:, 2, :].rearrange("p (t d) -> p t d", d=D),
                                        v16[:, 0, bass.ds(c * TPC, TPC), :],
                                        ALU.subtract).then_inc(s["qkv_lo_ready"], 1)

            def reduce_scores(n, item):
                dve.wait_ge(s["max_product"], n * RT + item + 1)
                nc.vector.reduce_max(max_parts[:, item % 4, item // 4:item // 4 + 1],
                                     max_ps[:, item % 2, :], AX_X).then_inc(s["max_reduced"], 1)

            statistics(0)
            variances(0)
            dve.wait_ge(s["weights_landed"], 16)
            nc.vector.reduce_max(absmax[:, 0:1], wqkv32[:], AX_XY, apply_absolute_value=True)
            dve.wait_ge(s["wo_landed"], 16)
            nc.vector.reduce_max(absmax[:, 1:2], wo32[:], AX_X, apply_absolute_value=True)
            dve.wait_ge(s["scales_landed"], 5 * 16)
            nc.vector.reduce_max(absmax[:, 2:3], bqkv_col[:], AX_X, apply_absolute_value=True)
            nc.vector.reduce_max(absmax[:, 3:4], gate_col[:], AX_XY, apply_absolute_value=True)
            nc.vector.reduce_max(absmax[:, 4:5], up_col[:], AX_XY, apply_absolute_value=True
                                 ).then_inc(s["absmax_ready"], 1)
            factors(0)
            dve.wait_ge(s["absmax_spread"], 1)
            nc.vector.tensor_scalar(bound[:, 0:2], absmax_all[:, 0:2], 2.0 ** -20, None, ALU.max)
            chain(nc.vector.scalar_tensor_tensor(bound[:, 2:3], absmax_all[:, 0:1], QKV_L1,
                                                 absmax_all[:, 2:3], ALU.mult, ALU.add))
            chain(nc.vector.tensor_scalar(bound[:, 3:4], absmax_all[:, 3:4], absmax_all[:, 4:5],
                                          FFN_L1 * FFN_L1, ALU.mult, ALU.mult))
            chain(nc.vector.tensor_scalar(bound[:, 2:4], bound[:, 2:4], 2.0 ** -20, None, ALU.max))
            chain(nc.vector.tensor_scalar(fit[:].bitcast(I32), bound[:].bitcast(I32), 0x7F800000, None,
                                          ALU.bitwise_and))
            nc.vector.tensor_scalar(fit[:].bitcast(I32), fit[:].bitcast(I32), -1.0, SCALE_BITS,
                                    ALU.mult, ALU.add).then_inc(s["fit_ready"], 1)
            dve.wait_ge(s["fit_ready"], 1)
            split_xn(0)
            for t in range(1, TPC):
                normalise(t)
            for t in range(1, TPC):
                split_xn(t)
            dve.wait_ge(s["w16_hi"], 1)
            nc.vector.scalar_tensor_tensor(wqkv16[:, 1, :, :], wqkv32[:], fit[:, 0:1],
                                           wqkv16[:, 0, :, :], ALU.mult, ALU.subtract
                                           ).then_inc(s["w16_ready"], 1)
            chain(nc.vector.tensor_scalar(unfit[:].bitcast(I32), fit[:].bitcast(I32), -1.0,
                                          INVERSE_BITS, ALU.mult, ALU.add))
            nc.vector.tensor_scalar(qkv_unscale[:], unfit[:, 0:1], fit[:, 2:3], 1.0 / X_SCALE,
                                    ALU.mult, ALU.mult)
            nc.vector.tensor_scalar(bqkv_sc[:], bqkv_col[:], fit[:, 2:3], None, ALU.mult
                                    ).then_inc(s["qkv_scales_ready"], 1)
            statistics(1)
            variances(1)
            factors(1)
            for t in range(TPC, 2 * TPC):
                normalise(t)
                split_xn(t)
            nc.vector.tensor_scalar(exp_scale[:], unfit[:, 2:3], unfit[:, 2:3], float(D) ** -0.5,
                                    ALU.mult, ALU.mult)
            nc.vector.tensor_scalar(shift_less[:], fit[:, 2:3], fit[:, 2:3],
                                    PROB_EXP * LN2 * float(D) ** 0.5, ALU.mult, ALU.mult)
            nc.vector.tensor_tensor(attn_unscale[:], unfit[:, 1:2], unfit[:, 2:3], ALU.mult)
            nc.vector.tensor_scalar(gate_dq[:], gate_col[:], 1.0 / X_SCALE, None, ALU.mult)
            nc.vector.tensor_scalar(up_dq[:], up_col[:], fit[:, 3:4], 1.0 / X_SCALE, ALU.mult, ALU.mult)
            nc.vector.tensor_scalar(down_dq[:], down_col[:], unfit[:, 3:4], None, ALU.mult
                                    ).then_inc(s["scales_ready"], 1)
            statistics(2)
            variances(2)
            factors(2)
            split_qk(0)
            split_v(0)
            split_xn(2 * TPC)
            statistics(3)
            split_xn(2 * TPC + 1)
            variances(3)
            split_xn(2 * TPC + 2)
            split_xn(2 * TPC + 3)
            factors(3)
            for t in range(TPC):
                reduce_scores(0, t)
            dve.wait_ge(s["wo16_hi"], 1)
            nc.vector.scalar_tensor_tensor(wo16[:, 1, :], wo32[:], fit[:, 1:2], wo16[:, 0, :],
                                           ALU.mult, ALU.subtract).then_inc(s["w16_ready"], 1)
            split_qk(1)
            split_v(1)
            for pair in ((0, 1), (2, 3)):
                for t in pair:
                    split_xn(3 * TPC + t)
                for t in pair:
                    reduce_scores(0, TPC + t)
            split_qk(2)
            split_v(2)
            for pair in ((0, 1), (2, 3)):
                for t in pair:
                    reduce_scores(0, 2 * TPC + t)
                split_qk(3, (pair[0] // 2,))
            for t in range(TPC):
                reduce_scores(0, 3 * TPC + t)

            def shift_of(n):
                dve.wait_ge(s["max_reduced"], (n + 1) * RT)
                nc.vector.reduce_max(max_col[:], max_parts[:], AX_X).then_inc(s["max_done"], 1)
                dve.wait_ge(s["max_done"], n + 1)
                nc.vector.tensor_scalar(max_less[:], max_col[:], shift_less[:, 0:1],
                                        -(2.0 ** -SHIFT_EXP), ALU.subtract, ALU.mult
                                        ).then_inc(s["max_moved"], 1)
                dve.wait_ge(s["max_moved"], n + 1)
                for j in range(TPC):
                    block_of = neg_max[:, bass.ds(n, 1), j * P:(j + 1) * P].rearrange("p a q -> p (a q)")
                    last = nc.vector.tensor_scalar(block_of, ident[:], max_less[:, j:j + 1], None,
                                                   ALU.mult)
                last.then_inc(s["shift_ready"], 1)

            def p_lo(n, k):
                dve.wait_ge(s["exp16_done"], n * RT + k + 1)
                nc.vector.tensor_tensor(p16[:, k % 4, 1, :], p32[:, k % 4, :], p16[:, k % 4, 0, :],
                                        ALU.subtract).then_inc(s["p_lo_ready"], 1)

            def split_sum(m):
                dve.wait_ge(s["p_summed"], (m + 1) * (RT - 1))
                nc.vector.tensor_copy(p_sum16[:, 0, :], p_sum[:]).then_inc(s["sum_hi_ready"], 1)
                dve.wait_ge(s["sum_hi_ready"], m + 1)
                nc.vector.tensor_tensor(p_sum16[:, 1, :], p_sum[:], p_sum16[:, 0, :], ALU.subtract
                                        ).then_inc(s["sum_split"], 1)

            def invert_sum(m, j):
                dve.wait_ge(s["sum_spread"], m + 1)
                part = slice(j * P, (j + 1) * P)
                nc.vector.reciprocal(inv_sum[:, part], tail_ps[:, part]).then_inc(s["sum_inverted"], 1)

            def scale_o(m):
                dve.wait_ge(s["o_copied"], m + 1)
                dve.wait_ge(s["sum_inverted"], (m + 1) * TPC)
                nc.vector.tensor_tensor(o_norm[:], o_raw[:], inv_sum[:], ALU.mult
                                        ).then_inc(s["o_scaled"], 1)

            def split_o(m):
                dve.wait_ge(s["o_hi_ready"], m + 1)
                nc.vector.tensor_tensor(o16[:, 1, :], o32[:], o16[:, 0, :], ALU.subtract
                                        ).then_inc(s["o_lo_ready"], 1)

            def attention(n, with_tail, with_next):
                item = 0
                for k in range(RT):
                    if with_next:
                        for _ in range(items_of(n)[k]):
                            reduce_scores(n + 1, item)
                            item += 1
                    p_lo(n, k)
                    if with_next and k == SHIFT_AT:
                        shift_of(n + 1)
                    if with_tail:
                        if k == 1:
                            split_sum(n - 1)
                        if INVERT_AT <= k < INVERT_AT + TPC:
                            invert_sum(n - 1, k - INVERT_AT)
                        if k == INVERT_AT + TPC:
                            scale_o(n - 1)
                        if k == INVERT_AT + TPC + 2:
                            split_o(n - 1)

            shift_of(0)
            split_v(NC - 1)
            attention(0, False, True)
            with dve.Fori(1, NC - 1) as n:
                attention(n, True, True)
            attention(NC - 1, True, False)

            def accumulate(t, item, dst, scale):
                at = order_of(t).index(item)
                dve.wait_ge(s["ffn_product"], products_before(t) + at + 1)
                dst = dst.rearrange("p (a b) -> p a b", b=CHUNK)
                nc.vector.scalar_tensor_tensor(dst, ffn_ps[:, slot_of(t, at), :, :], scale,
                                               dst, ALU.mult, ALU.add).then_inc(s["dve_drained"], 1)

            def make_h(t, parity):
                dve.wait_ge(s["silu_done"], t + 1)
                if first(t):
                    dve.wait_ge(s["opening_added"], 2)
                else:
                    dve.wait_ge(s["dve_drained"], dve_drains_before(t + 1))
                if not (isinstance(t, int) and t < 2):
                    dve.wait_ge(s["h_lo_ready"], t - 1)
                nc.vector.tensor_tensor(h32[:, parity, :], silu32[:], u32[:, parity, :], ALU.mult
                                        ).then_inc(s["h_ready"], 1)

            def add_gate(t, parity, tile, g, done):
                if g == 1:
                    dve.wait_ge(s["act_drained"], act_drains_before(t) + 1)
                else:
                    dve.wait_ge(s["dve_drained"], done + 2 * g - 3)
                accumulate(t, ("g", g), g32[:, parity, :], gate_dq[:, bass.ds(tile, 1), g])

            def add_up(t, parity, tile, g, done):
                if g == 1:
                    dve.wait_ge(s["act_drained"], act_drains_before(t) + 2)
                else:
                    dve.wait_ge(s["dve_drained"], done + 2 * g - 2)
                accumulate(t, ("u", g), u32[:, parity, :], up_dq[:, bass.ds(tile, 1), g])

            def final_scale(half, j, parts=(0, 1)):
                dve.wait_ge(s["final_silu"], half * HT + j + 1)
                for part in parts:
                    rows = slice(half * HALF + part * CHUNK, half * HALF + (part + 1) * CHUNK)
                    ys = ysum[:, bass.ds(j, 1), rows]
                    nc.vector.tensor_tensor(ys, ys, attnT[:, bass.ds(j, 1), rows], ALU.mult
                                            ).then_inc(s["final_scaled"], 1)

            def ffn_step(t, parity, tile, y_tile, half, final=None):
                rows = slice(half * HALF, (half + 1) * HALF)
                if isinstance(t, int) and t == 2:
                    dve.wait_ge(s["ysum_zeroed"], 1)
                else:
                    dve.wait_ge(s["dve_drained"], dve_drains_before(t) - 6)
                accumulate(t, ("y", 0), ysum[:, 0, rows], down_dq[:, 0, bass.ds(y_tile, 1)])
                for g in range(1, HT):
                    add_gate(t, parity, tile, g, dve_drains_before(t) + 1)
                    add_up(t, parity, tile, g, dve_drains_before(t) + 1)
                if final is not None:
                    final_scale(0, final[0], (final[1],))
                make_h(t, parity)

            split_sum(NC - 1)
            for j in range(3):
                invert_sum(NC - 1, j)
            add_gate(0, 0, 0, 1, 0)
            invert_sum(NC - 1, 3)
            add_up(0, 0, 0, 1, 0)
            scale_o(NC - 1)
            add_gate(0, 0, 0, 2, 0)
            add_up(0, 0, 0, 2, 0)
            done = dve_drains_before(1)
            split_o(NC - 1)
            add_gate(1, 1, 1, 1, done)
            add_up(1, 1, 1, 1, done)
            make_h(0, 0)
            for g in range(2, HT):
                add_gate(1, 1, 1, g, done)
                add_up(1, 1, 1, g, done)
            make_h(1, 1)
            ffn_step(2, 0, 2, 0, 0)
            ffn_step(3, 1, 3, 1, 0)
            with dve.Fori(2, OT // 2) as pair:
                ffn_step(pair * 2, 0, pair * 2, pair * 2 - 2, 0)
                ffn_step(pair * 2 + 1, 1, pair * 2 + 1, pair * 2 - 1, 0)
            ffn_step(OT, 0, 0, OT - 2, 0)
            ffn_step(OT + 1, 1, 1, OT - 1, 0)
            ffn_step(OT + 2, 0, 2, 0, 1)
            ffn_step(OT + 3, 1, 3, 1, 1)
            with dve.Fori(0, HT) as j:
                ffn_step(j * 2 + OT + 4, 0, j * 2 + 4, j * 2 + 2, 1, final=(j, 0))
                ffn_step(j * 2 + OT + 5, 1, j * 2 + 5, j * 2 + 3, 1, final=(j, 1))
            ffn_step(STEPS - 2, 0, OT - 2, OT - 4, 1)
            ffn_step(STEPS - 1, 1, OT - 1, OT - 3, 1)
            rows = slice((NH - 1) * HALF, NH * HALF)

            def close(product, j, tile, sums):
                dve.wait_ge(s["ffn_product"], products_before(STEPS) + product + 1)
                dve.wait_ge(s[sums[0]], sums[1])
                dst = ysum[:, j, rows].rearrange("p (a b) -> p a b", b=CHUNK)
                nc.vector.scalar_tensor_tensor(dst, ffn_ps[:, j, :, :], down_dq[:, j, tile:tile + 1],
                                               dst, ALU.mult, ALU.add).then_inc(s["dve_drained"], 1)

            done = dve_drains_before(STEPS)
            close(0, 0, OT - 2, ("dve_drained", done - 6))
            dve.wait_ge(s["h_hi_ready"], STEPS)
            nc.vector.tensor_tensor(h16[:, 1, 1, :], h32[:, 1, :], h16[:, 1, 0, :], ALU.subtract
                                    ).then_inc(s["last_h_lo_ready"], 1)
            close(1, 1, OT - 2, ("y_added", 3 * (STEPS - 3) + 1))
            summed = 3 * (STEPS - 2)
            close(4, 0, OT - 1, ("dve_drained", done + 1))
            close(5, 1, OT - 1, ("dve_drained", done + 2))
            final_scale(NH - 1, 0)
            close(6, 2, OT - 1, ("y_added", summed + 1))
            final_scale(NH - 1, 1)
            close(7, 3, OT - 1, ("y_added", summed + 2))
            final_scale(NH - 1, 2)
            final_scale(NH - 1, 3)
            dve.wait_ge(s["residual_landed"], 16 * NH)
            for j, part in DVE_LAST:
                dve.wait_ge(s["final_scaled"], ((NH - 1) * HT + j) * 2 + part + 1)
                add_residual(nc.vector, j, part).then_inc(s["last_ready"], 1)

        @block.tensor
        def _(pe):
            PAIRS = ((0, 0), (0, 1), (1, 0))

            def transpose_xn(c, t):
                if not (isinstance(c, int) and c * TPC + t < 2):
                    pe.wait_ge(s["xn_stored"], c * TPC + t - 1)
                pe.wait_ge(s["xn_lo_ready"], c * TPC + t + 1)
                for part in range(2):
                    for i in range(HT):
                        last = nc.tensor.transpose(
                            xn_ps[:, t % 2, part, i, :],
                            xn16[:, (c * TPC + t) % (2 * TPC), part, i * P:(i + 1) * P], ident[:])
                last.then_inc(s["xn_transposed"], 1)

            def project_qk(c, of=(0, 1)):
                pe.wait_ge(s["xn_stored"], (c + 1) * TPC)
                for n in of:
                    w0 = (D, 0)[n]
                    if not first(c):
                        pe.wait_ge(s["qkv32_ready"], c * 3 - 2 + n)
                    for i in range(HT):
                        for w, a in PAIRS:
                            last = nc.tensor.matmul(qkv_ps[:, n, :], wqkv16[:, w, i, w0:w0 + D],
                                                    xnT[:, a, i, bass.ds(c * CHUNK, CHUNK)],
                                                    start=(i == 0 and (w, a) == (0, 0)),
                                                    stop=(i == HT - 1 and (w, a) == (1, 0)))
                    last.then_inc(s[("k_product", "q_product")[n]], 1)

            def project_v(c, tiles):
                if not first(c) and tiles[0] == 0:
                    pe.wait_ge(s["qkv32_ready"], c * 3)
                for t in tiles:
                    for i in range(HT):
                        for a, w in PAIRS:
                            last = nc.tensor.matmul(qkv_ps[:, 2, t * D:(t + 1) * D],
                                                    xnT[:, a, i, bass.ds(c * CHUNK + t * P, P)],
                                                    wqkv16[:, w, i, 2 * D:3 * D],
                                                    start=(i == 0 and (a, w) == (0, 0)),
                                                    stop=(i == HT - 1 and (a, w) == (1, 0)))
                if tiles[-1] == TPC - 1:
                    last.then_inc(s["v_product"], 1)

            def max_scores(n, item):
                if not (isinstance(n, int) and n == 0 and item < 2):
                    pe.wait_ge(s["max_reduced"], n * RT + item - 1)
                q0, key0 = n * CHUNK + (item % 4) * P, (item // 4) * CHUNK
                nc.tensor.matmul(max_ps[:, item % 2, :], q16[:, 0, bass.ds(q0, P)],
                                 k16[:, 0, key0:key0 + CHUNK],
                                 start=True, stop=True).then_inc(s["max_product"], 1)

            def keep_busy(products):
                for _ in range(products):
                    nc.tensor.matmul(tail_ps[:, 0:P], ones16[:], ones16[:], start=True, stop=True)

            pe.wait_ge(s["identity_ready"], 1)
            pe.wait_ge(s["consts_ready"], 1)
            pe.wait_ge(s["absmax_spread"], 1)
            keep_busy(28)
            for t in range(TPC):
                transpose_xn(0, t)
                keep_busy(6)
            pe.wait_ge(s["w16_ready"], 1)
            for c in range(NC - 1):
                project_qk(c)
                if c == 1:
                    project_v(1, (0, 1))
                    transpose_xn(2, 0)
                    transpose_xn(2, 1)
                    project_v(1, (2,))
                    transpose_xn(2, 2)
                    transpose_xn(2, 3)
                    max_scores(0, 0)
                    max_scores(0, 1)
                    project_v(1, (3,))
                    max_scores(0, 2)
                    max_scores(0, 3)
                    continue
                for pair in ((0, 1), (2, 3)):
                    if c == 0:
                        project_v(0, pair)
                    for t in pair:
                        transpose_xn(c + 1, t)
                    if c > 1:
                        for t in pair:
                            max_scores(0, (c - 1) * TPC + t)
                        project_v(c, pair)
            for n, pair in enumerate(((0, 1), (2, 3))):
                project_qk(NC - 1, (n,))
                for t in pair:
                    max_scores(0, (NC - 2) * TPC + t)
            for pair in ((0, 1), (2, 3)):
                project_v(NC - 1, pair)
                pe.wait_ge(s["qkv_hi_ready"], (NC - 1) * 3 + 1)
                for t in pair:
                    max_scores(0, (NC - 1) * TPC + t)

            pe.wait_ge(s["consts_ready"], 1)
            pe.wait_ge(s["qkv_lo_ready"], 3 * NC - 1)
            pe.wait_ge(s["w16_ready"], 2)

            def scores(n, k):
                if not first(n) or k >= 4:
                    pe.wait_ge(s["exp16_done"], n * RT + k - 3)
                for i, (a, b) in enumerate(PAIRS):
                    nc.tensor.matmul(score_ps[:, k % 4, :], k16[:, a, k * P:(k + 1) * P],
                                     q16[:, b, bass.ds(n * CHUNK, CHUNK)], start=(i == 0), stop=False)

            def subtract_maximum(n, k):
                if k == 0:
                    pe.wait_ge(s["shift_ready"], n + 1)
                nc.tensor.matmul(score_ps[:, k % 4, :], shift_up[:],
                                 neg_max[:, bass.ds(n, 1), :].rearrange("p a q -> p (a q)"),
                                 start=False, stop=True).then_inc(s["score_product"], 1)

            def weighted_values(n, k):
                if k == 0 and first(n):
                    pe.wait_ge(s["qkv_lo_ready"], 3 * NC)
                pe.wait_ge(s["p_lo_ready"], n * RT + k + 1)
                if k == 0 and not first(n):
                    pe.wait_ge(s["o_copied"], n)
                for i, (a, b) in enumerate(PAIRS):
                    last = nc.tensor.matmul(o_ps[:], v16[:, a, k, :], p16[:, k % 4, b, :],
                                            start=(k == 0 and i == 0), stop=(k == RT - 1 and i == 2))
                last.then_inc(s["pv_product"], 1)

            def spread_sum(m):
                pe.wait_ge(s["sum_split"], m + 1)
                if isinstance(m, int) and m > 0:
                    pe.wait_ge(s["attn_stored"], m * HT)
                for part in range(2):
                    last = nc.tensor.matmul(tail_ps[:], ones16[:], p_sum16[:, part, :],
                                            start=(part == 0), stop=(part == 1))
                last.then_inc(s["sum_spread"], 1)

            def attention_out(m, j):
                if j == 0:
                    pe.wait_ge(s["o_lo_ready"], m + 1)
                else:
                    pe.wait_ge(s["attn_stored"], m * HT + j)
                for i, (a, b) in enumerate(PAIRS):
                    last = nc.tensor.matmul(tail_ps[:], wo16[:, a, j * P:(j + 1) * P], o16[:, b, :],
                                            start=(i == 0), stop=(i == 2))
                last.then_inc(s["attn_product"], 1)

            def attention(n, with_previous, with_next):
                item = 0
                for k in range(RT):
                    if k >= LAG:
                        weighted_values(n, k - LAG)
                    elif with_previous:
                        weighted_values(n - 1, RT + k - LAG)
                    if first(n) and k == 0:
                        for ahead in range(4):
                            scores(n, ahead)
                    elif not first(n) or k >= 4:
                        scores(n, k)
                    subtract_maximum(n, k)
                    if with_next:
                        for _ in range(items_of(n)[k]):
                            max_scores(n + 1, item)
                            item += 1
                    if with_previous:
                        if k == INVERT_AT - 1:
                            spread_sum(n - 1)
                        if k >= OUT_AT:
                            attention_out(n - 1, k - OUT_AT)

            attention(0, False, True)
            with pe.Fori(1, NC - 1) as n:
                attention(n, True, True)
            attention(NC - 1, True, False)
            for k in range(RT - LAG, RT):
                weighted_values(NC - 1, k)

            def drained(t, at):
                order, by_act = order_of(t), act_drains_of(t)
                item = order[at]
                if item in by_act:
                    pe.wait_ge(s["act_drained"], act_drains_before(t) + by_act.index(item) + 1)
                else:
                    own = [x for x in order if x not in by_act].index(item)
                    pe.wait_ge(s["dve_drained"], dve_drains_before(t) + own + 1)

            def gate_up_product(t, at, tile, rows):
                kind, g = order_of(t)[at]
                w16 = gate16 if kind == "g" else up16
                for half in range(2):
                    r0 = rows + half * CHUNK
                    for part in range(2):
                        last = nc.tensor.matmul(ffn_ps[:, slot_of(t, at), half, :],
                                                w16[:, g, bass.ds(tile * P, P)],
                                                xnT[:, part, g, r0:r0 + CHUNK],
                                                start=(part == 0), stop=(part == 1))
                last.then_inc(s["ffn_product"], 1)

            def down_product(slot, j, tile, h_parity):
                for half in range(2):
                    for part in range(2):
                        last = nc.tensor.matmul(
                            ffn_ps[:, slot, half, :],
                            down16[:, bass.ds(tile, 1), j * P:(j + 1) * P].rearrange("p a b -> p (a b)"),
                            h16[:, h_parity, part, half * CHUNK:(half + 1) * CHUNK],
                            start=(part == 0), stop=(part == 1))
                last.then_inc(s["ffn_product"], 1)

            def opening_step(t, at):
                n = t * len(OPEN[0]) + at - (RING - 1)
                if n >= 0:
                    drained(n // len(OPEN[0]), n % len(OPEN[0]))
                gate_up_product(t, at, t, 0)

            def ffn_step(t, parity, tile, y_tile, rows):
                for at in range(len(FULL)):
                    if at >= RING:
                        drained(t, at - RING)
                    elif isinstance(t, int) and t == 2:
                        if at < RING - 1:
                            drained(1, len(OPEN[1]) - (RING - 1) + at)
                        else:
                            pe.wait_ge(s["attn_stored"], NC * HT)
                    else:
                        drained(t - 1, len(FULL) + at - RING)
                    kind, j = FULL[at]
                    if kind != "y":
                        gate_up_product(t, at, tile, rows)
                        continue
                    if j == 0:
                        pe.wait_ge(s["h_lo_ready"], t - 1)
                    down_product(at % RING, j, y_tile, parity)

            pe.wait_ge(s["int4_landed"], 3 * 16)
            pe.wait_ge(s["exp16_done"], NC * RT)
            spread_sum(NC - 1)
            pe.wait_ge(s["o_copied"], NC)
            for at in range(len(OPEN[0])):
                opening_step(0, at)
            for at in range(4):
                opening_step(1, at)
            for j in range(HT):
                attention_out(NC - 1, j)
                opening_step(1, 4 + j)
            ffn_step(2, 0, 2, 0, 0)
            ffn_step(3, 1, 3, 1, 0)
            with pe.Fori(2, OT // 2) as pair:
                ffn_step(pair * 2, 0, pair * 2, pair * 2 - 2, 0)
                ffn_step(pair * 2 + 1, 1, pair * 2 + 1, pair * 2 - 1, 0)
            ffn_step(OT, 0, 0, OT - 2, HALF)
            ffn_step(OT + 1, 1, 1, OT - 1, HALF)
            with pe.Fori(OT // 2 + 1, OT) as pair:
                ffn_step(pair * 2, 0, pair * 2 - OT, pair * 2 - OT - 2, HALF)
                ffn_step(pair * 2 + 1, 1, pair * 2 + 1 - OT, pair * 2 - OT - 1, HALF)
            for j in range(HT):
                if j == 0:
                    pe.wait_ge(s["h_lo_ready"], STEPS - 1)
                drained(STEPS - 1, len(FULL) + j - RING)
                down_product(j, j, OT - 2, 0)
            pe.wait_ge(s["last_h_lo_ready"], 1)
            for j in range(HT):
                if j < 2:
                    pe.wait_ge(s["dve_drained"], dve_drains_before(STEPS) + j + 1)
                else:
                    pe.wait_ge(s["act_drained"], act_drains_before(STEPS) + j - 1)
                down_product(j, j, OT - 1, 1)


def kernel(L0_attn_x, L0_attn_Wqkv, L0_attn_bqkv, L0_attn_Wo, L0_attn_bo, L0_ffn_gate_q,
           L0_ffn_gate_s, L0_ffn_up_q, L0_ffn_up_s, L0_ffn_down_q, L0_ffn_down_s):
    import numpy as np
    import concourse.bacc as bacc
    from concourse.bass_utils import run_bass_kernel_spmd

    def columns(a, width):
        a = np.asarray(a).reshape(-1, P, width)
        return a.transpose(1, 0, 2)

    def grouped(q):
        q = np.asarray(q)
        return q.T.reshape(-1, P, q.shape[0]).transpose(1, 0, 2)

    x = np.asarray(L0_attn_x)[0]
    arrays = {
        "x": x, "xT": x.T, "wqkv": L0_attn_Wqkv,
        "bqkv": columns(L0_attn_bqkv, 1)[:, :, 0], "wo": L0_attn_Wo,
        "bo": columns(L0_attn_bo, 1)[:, :, 0],
        "gate_q": grouped(L0_ffn_gate_q), "gate_s": columns(L0_ffn_gate_s, HT),
        "up_q": grouped(L0_ffn_up_q), "up_s": columns(L0_ffn_up_s, HT),
        "down_q": grouped(L0_ffn_down_q), "down_s": columns(L0_ffn_down_s, OT),
    }
    arrays = {name: np.ascontiguousarray(a) for name, a in arrays.items()}
    nc = bacc.Bacc("TRN2", target_bir_lowering=False, num_devices=1)
    args = [nc.dram_tensor(name, a.shape, mybir.dt.from_np(a.dtype), kind="ExternalInput").ap()
            for name, a in arrays.items()]
    out = nc.dram_tensor("outT", (HID, ROWS), F32, kind="ExternalOutput").ap()
    build(nc, *args, out)
    result = run_bass_kernel_spmd(nc, [arrays], core_ids=[0])
    return np.asarray(result.results[0]["outT"]).T[None]
```
